# Optimizing a Trainium2 kernel written in Bass

```python
import numpy as np
import jax
import jax.numpy as jnp

def _softmax(x, axis=-1):
    return jax.nn.softmax(x, axis=axis)

def _gelu(x):
    return jax.nn.gelu(x, approximate=True)

def _silu(x):
    return jax.nn.silu(x)

def _sigmoid(x):
    return jax.nn.sigmoid(x)

def _layernorm(x, axis=-1, eps=1e-05):
    m = jnp.mean(x, axis=axis, keepdims=True)
    v = jnp.var(x, axis=axis, keepdims=True)
    return (x - m) / jnp.sqrt(v + eps)

def _scatter_add(tgt, idx, src, axis=0):
    return tgt.at[idx].add(src)

def _segment_sum(src, seg, n):
    return jax.ops.segment_sum(src, seg, n)
kernel_name = 'mk_cond_resid_d2_seqx_r8_0a5937'

def setup_inputs(seed: int=0):
    np.random.seed(seed)
    _w = jnp.asarray

    def _rec_inputs():
        import jax
        import jax.numpy as jnp
        _rk = jax.random.key(seed)
        x = -0.000125 + 0.9999 * jax.random.normal(jax.random.fold_in(_rk, 1), (128, 32, 512), jnp.float32)
        _lenS = 32 - jax.random.randint(jax.random.fold_in(_rk, 7), (128,), 0, max(1, 32 // 4) + 1, jnp.int32)
        _lenS2 = 32 - jax.random.randint(jax.random.fold_in(_rk, 8), (128,), 0, max(1, 32 // 4) + 1, jnp.int32)
        itok_B_0_7 = jax.random.randint(jax.random.fold_in(_rk, 11), (128,), 0, 8, jnp.int32)
        itok_B_2_6 = jax.random.randint(jax.random.fold_in(_rk, 12), (128,), 2, 7, jnp.int32)
        return (x, itok_B_0_7, itok_B_2_6)
    x, itok_B_0_7, itok_B_2_6 = _rec_inputs()

    def _L0_cond_setup():
        import jax, jax.numpy as jnp
        import numpy as np
        TOP_K = 2
        LANG_BIAS = 5.0
        SCALING = 32.0 / 16.0
        LANGUAGE_PAD_ID = -1
        key = jax.random.key(seed)
        ks = jax.random.split(key, 6)
        B, T, D, O, E, R = (4, 256, 512, 512, 8, 16)
        x = jax.random.normal(ks[0], (B, T, D), dtype=jnp.float32)
        language_ids = jax.random.randint(ks[1], (B,), 0, E).astype(jnp.int64)
        W = jax.random.normal(ks[2], (O, D), dtype=jnp.float32) * (1.0 / np.sqrt(D))
        Wr = jax.random.normal(ks[3], (E, D), dtype=jnp.float32) * (1.0 / np.sqrt(D))
        A = jax.random.normal(ks[4], (E, R, D), dtype=jnp.float32) * (1.0 / np.sqrt(D))
        Bm = jax.random.normal(ks[5], (O, R), dtype=jnp.float32) * 0.0
        Bm = jnp.broadcast_to(Bm, (E, O, R)) + jax.random.normal(ks[5], (E, O, R), dtype=jnp.float32) * 0.02
        return {'x': x, 'language_ids': language_ids, 'W': W, 'Wr': Wr, 'A': A, 'B': Bm}
    _L0_cond_all = _L0_cond_setup()
    _L0_cond_in = {k: v for k, v in _L0_cond_all.items() if k in ('W', 'Wr', 'A', 'B')}
    del _L0_cond_all

    def _L1_cond_setup():
        import jax, jax.numpy as jnp
        import numpy as np
        B, N, H, F = (4, 64, 512, 1376)
        L, R, RANK = (1, 16, 16)
        SCALE = 0.5
        key = jax.random.key(seed)
        ks = jax.random.split(key, 12)
        nrm = lambda k, shape, fan: jax.random.normal(k, shape, jnp.float32) * fan ** (-0.5)
        inp = {'x': jax.random.normal(ks[0], (B, N, H), jnp.float32), 'W_gate': nrm(ks[1], (F, H), H), 'W_up': nrm(ks[2], (F, H), H), 'W_down': nrm(ks[3], (H, F), F), 'A_gate': nrm(ks[4], (L, R, RANK, H), H), 'B_gate': nrm(ks[5], (L, R, F, RANK), RANK), 'A_up': nrm(ks[6], (L, R, RANK, H), H), 'B_up': nrm(ks[7], (L, R, F, RANK), RANK), 'A_down': nrm(ks[8], (L, R, RANK, F), F), 'B_down': nrm(ks[9], (L, R, H, RANK), RANK), 'lora_indices': jax.random.randint(ks[10], (B,), 0, R), 'layer_idx': 0}
        return inp
    _L1_cond_all = _L1_cond_setup()
    _L1_cond_in = {k: v for k, v in _L1_cond_all.items() if k in ('W_gate', 'W_up', 'W_down', 'A_gate', 'B_gate', 'A_up', 'B_up', 'A_down', 'B_down')}
    del _L1_cond_all
    return {'x': x, 'itok_B_0_7': itok_B_0_7, 'itok_B_2_6': itok_B_2_6, 'L0_cond_W': _L0_cond_in['W'], 'L0_cond_Wr': _L0_cond_in['Wr'], 'L0_cond_A': _L0_cond_in['A'], 'L0_cond_B': _L0_cond_in['B'], 'L1_cond_W_gate': _L1_cond_in['W_gate'], 'L1_cond_W_up': _L1_cond_in['W_up'], 'L1_cond_W_down': _L1_cond_in['W_down'], 'L1_cond_A_gate': _L1_cond_in['A_gate'], 'L1_cond_B_gate': _L1_cond_in['B_gate'], 'L1_cond_A_up': _L1_cond_in['A_up'], 'L1_cond_B_up': _L1_cond_in['B_up'], 'L1_cond_A_down': _L1_cond_in['A_down'], 'L1_cond_B_down': _L1_cond_in['B_down']}

def reference(x, itok_B_0_7, itok_B_2_6, L0_cond_W, L0_cond_Wr, L0_cond_A, L0_cond_B, L1_cond_W_gate, L1_cond_W_up, L1_cond_W_down, L1_cond_A_gate, L1_cond_B_gate, L1_cond_A_up, L1_cond_B_up, L1_cond_A_down, L1_cond_B_down):
    import jax
    import jax.numpy as jnp

    def _L0_cond_ref(x, language_ids, W, Wr, A, B):
        import jax, jax.numpy as jnp
        import numpy as np
        TOP_K = 2
        LANG_BIAS = 5.0
        SCALING = 32.0 / 16.0
        LANGUAGE_PAD_ID = -1
        base = jnp.einsum('btd,od->bto', x, W)
        E = Wr.shape[0]
        logits = jnp.einsum('btd,ed->bte', x.astype(jnp.float32), Wr.astype(jnp.float32))
        expert_targets = language_ids
        valid = expert_targets >= 0
        tgt = jnp.where(valid, expert_targets, 0)
        bias = jax.nn.one_hot(tgt, E, dtype=logits.dtype) * LANG_BIAS
        bias = jnp.where(valid[:, None], bias, 0.0)
        logits = logits + bias[:, None, :]
        topw, topi = jax.lax.top_k(logits, TOP_K)
        weights = jax.nn.softmax(topw, axis=-1)
        gates = jnp.sum(jax.nn.one_hot(topi, E, dtype=weights.dtype) * weights[..., None], axis=-2)
        gates = gates.astype(x.dtype)
        h = jnp.einsum('btd,erd->bter', x, A)
        lora_out = jnp.einsum('bter,bte,eor->bto', h, gates, B)
        return base + SCALING * lora_out

    def _L1_cond_ref(x, W_gate, W_up, W_down, A_gate, B_gate, A_up, B_up, A_down, B_down, lora_indices, layer_idx):
        import jax, jax.numpy as jnp
        import numpy as np
        B, N, H, F = (4, 64, 512, 1376)
        L, R, RANK = (1, 16, 16)
        SCALE = 0.5

        def lora_add(base, inp, A, B):
            Ab = A[layer_idx][lora_indices]
            Bb = B[layer_idx][lora_indices]
            t = jnp.einsum('bri,bni->bnr', Ab, inp)
            return base + jnp.einsum('bor,bnr->bno', Bb, t) * SCALE
        gate = lora_add(jnp.einsum('bnh,fh->bnf', x, W_gate), x, A_gate, B_gate)
        up = lora_add(jnp.einsum('bnh,fh->bnf', x, W_up), x, A_up, B_up)
        act = jax.nn.silu(gate) * up
        down = lora_add(jnp.einsum('bnf,hf->bnh', act, W_down), act, A_down, B_down)
        return down
    x = x + _L0_cond_ref(x, itok_B_0_7, L0_cond_W, L0_cond_Wr, L0_cond_A, L0_cond_B)
    x = x + _L1_cond_ref(x, L1_cond_W_gate, L1_cond_W_up, L1_cond_W_down, L1_cond_A_gate, L1_cond_B_gate, L1_cond_A_up, L1_cond_B_up, L1_cond_A_down, L1_cond_B_down, itok_B_2_6, 0)
    return x

_drawn_inputs = setup_inputs


def setup_inputs(seed=0):
    import zlib

    import numpy as np

    out = dict(_drawn_inputs(seed))
    spreads = {}
    factors = {'L0_cond_Wr': 4.001}
    for name, (base, spread) in spreads.items():
        noise = np.random.default_rng([zlib.crc32(name.encode()), seed]).standard_normal(out[name].shape)
        drawn = base * np.exp(spread * noise) if base else spread * noise
        out[name] = jnp.asarray(drawn.astype(out[name].dtype))
    for name, factor in factors.items():
        out[name] = (out[name] * factor).astype(out[name].dtype)
    return out
```

```python
from contextlib import ExitStack

import concourse.bass as bass
from concourse import mybir

ALU = mybir.AluOpType
ACT = mybir.ActivationFunctionType
AX_X = mybir.AxisListType.X
F32 = mybir.dt.float32
I32 = mybir.dt.int32

P = 128
BATCH, SEQ, D = 128, 32, 512
TOK = BATCH * SEQ
E0, R0 = 8, 16
E1, R1 = 16, 16
F = 1376
NF = -(-F // P)
FP = NF * P
KD = D // P
N = 512
NCH = TOK // N
SUB = N // P
BPC = N // SEQ
HB = BPC // 2
HN = N // 2
LANG_BIAS, SCALING, LORA_SCALE = 5.0, 2.0, 0.5


def build(nc, xT, lang, adapter, w0, a0, b0, wr, w1, agu, bgu, adn, bdn, outT):
    x1_dram = nc.dram_tensor("x1_scratch", (D, TOK), F32, kind="Internal").ap()
    x_v = xT.rearrange("(k p) t -> p k t", p=P)
    x1_v = x1_dram.rearrange("(k p) t -> p k t", p=P)
    out_v = outT.rearrange("(k p) t -> p k t", p=P)

    def after(eng, semaphore, n):
        if not isinstance(n, int) or n > 0:
            eng.wait_ge(semaphore, n)

    with ExitStack() as ctx:
        def sb(name, shape, dt=F32):
            return ctx.enter_context(nc.sbuf_tensor(name, shape, dt))

        def sem(name):
            return ctx.enter_context(nc.semaphore(name))

        w0_sb = sb("w0_sb", [P, KD, D])
        a0_sb = sb("a0_sb", [P, KD, P])
        b0_sb = sb("b0_sb", [P, D])
        wr_sb = sb("wr_sb", [P, KD, E0])
        x_in = sb("x_in", [P, KD, N])
        x_w = sb("x_w", [P, KD, N])
        x1_out = sb("x1_out", [P, KD, N])
        h_sb = sb("h_sb", [P, N])
        hg_sb = sb("hg_sb", [P, N])
        logitT = sb("logitT", [E0, N])
        ident = sb("ident", [P, P])
        lower = sb("lower", [P, E0, E0])
        lang_sb = sb("lang_sb", [P, NCH * SUB], I32)
        expert_no = sb("expert_no", [P, E0], I32)
        bias = sb("bias", [P, NCH * SUB, E0])
        logit = sb("logit", [P, SUB, E0])
        top = sb("top", [P, SUB])
        ex = sb("ex", [P, SUB, E0])
        above = sb("above", [P, SUB, E0, E0])
        tied = sb("tied", [P, SUB, E0, E0])
        rank = sb("rank", [P, SUB, E0])
        den = sb("den", [P, SUB])
        gate_rows = sb("gate_rows", [P, SUB, E0, R0])
        w1_sb = sb("w1_sb", [P, NF, 3, D])
        agu_sb = sb("agu_sb", [P, BPC, KD, 2, R1])
        agu_w = sb("agu_w", [P, KD * 2, BPC, R1])
        adn_w = sb("adn_w", [P, NF, BPC, R1])
        bgu_sb = sb("bgu_sb", [P, 2, NF, 2, P])
        adn_sb = sb("adn_sb", [P, BPC, NF, R1])
        bdn_sb = sb("bdn_sb", [P, 2, D])
        own = sb("own", [P, 2, HB, SEQ])
        y_in = sb("y_in", [P, KD, N])
        y_w = x_w
        t_gu = sb("t_gu", [P, 2, N])
        t_dn = sb("t_dn", [P, N])
        silu = sb("silu", [P, 2, N])
        act_sb = sb("act_sb", [P, 2, N])
        y_out = x1_out
        adapter_sb = sb("adapter_sb", [1, BATCH], I32)

        acc = ctx.enter_context(nc.psum_tensor("acc", [P, KD, N], F32))
        rot = ctx.enter_context(nc.psum_tensor("rot", [P, 3, N], F32))
        aux = ctx.enter_context(nc.psum_tensor("aux", [P, N], F32))

        weights0_in = sem("weights0_in")
        weights1_in = sem("weights1_in")
        lang_in = sem("lang_in")
        adapter_in = sem("adapter_in")
        consts_step = sem("consts_step")
        consts_done = sem("consts_done")
        x_landed = sem("x_landed")
        x_taken = sem("x_taken")
        h_ready = sem("h_ready")
        logitT_ready = sem("logitT_ready")
        h_copied = sem("h_copied")
        logitT_copied = sem("logitT_copied")
        logit_ready = sem("logit_ready")
        gate_step = sem("gate_step")
        shifted = sem("shifted")
        ex_ready = sem("ex_ready")
        gates_ready = sem("gates_ready")
        gates_turned = sem("gates_turned")
        hg_ready = sem("hg_ready")
        l0_ready = sem("l0_ready")
        x1_ready = sem("x1_ready")
        x1_stored = sem("x1_stored")
        y_landed = sem("y_landed")
        y_taken = sem("y_taken")
        agu_landed = sem("agu_landed")
        bgu_landed = sem("bgu_landed")
        adn_landed = sem("adn_landed")
        bdn_landed = sem("bdn_landed")
        agu_packed = sem("agu_packed")
        adn_packed = sem("adn_packed")
        tgu_summed = sem("tgu_summed")
        tgu_ready = sem("tgu_ready")
        gate_summed = sem("gate_summed")
        up_summed = sem("up_summed")
        silu_ready = sem("silu_ready")
        act_ready = sem("act_ready")
        down_step = sem("down_step")
        tdn_summed = sem("tdn_summed")
        tdn_ready = sem("tdn_ready")
        out_summed = sem("out_summed")
        out_ready = sem("out_ready")
        out_stored = sem("out_stored")

        block = ctx.enter_context(nc.Block())

        @block.sync
        def _(sp):
            sp.dma_start(x_in[:], x_v[:, :, 0:N]).then_inc(x_landed, 16)
            sp.dma_start(a0_sb[:], a0).then_inc(weights0_in, 16)
            sp.dma_start(wr_sb[:], wr).then_inc(weights0_in, 16)
            sp.dma_start(w0_sb[:], w0).then_inc(weights0_in, 16)
            sp.dma_start(b0_sb[:], b0).then_inc(weights0_in, 16)
            sp.dma_start(adapter_sb[:], adapter).then_inc(adapter_in, 16)
            for j in range(P // SEQ):
                sp.dma_start(lang_sb[SEQ * j:SEQ * (j + 1), :],
                             lang[j:j + 1].to_broadcast([SEQ, NCH * SUB])).then_inc(lang_in, 16)
            for f in range(NF):
                sp.dma_start(w1_sb[:, f], w1[f]).then_inc(weights1_in, 16)
            with sp.Fori(1, NCH) as c:
                after(sp, x_taken, c)
                sp.dma_start(x_in[:], x_v[:, :, bass.ds(c * N, N)]).then_inc(x_landed, 16)
            sp.wait_ge(adapter_in, 16)
            def load(c):
                sp.wait_ge(x1_stored, 16 * NCH)
                after(sp, y_taken, c)
                sp.dma_start(y_in[:], x1_v[:, :, bass.ds(c * N, N)]).then_inc(y_landed, 16)
                after(sp, out_summed, c)
                for b in range(BPC):
                    e = sp.value_load(adapter_sb[0:1, bass.ds(c * BPC + b, 1)], min_val=0, max_val=E1 - 1)
                    rows = slice(R1 * (b % HB), R1 * (b % HB + 1))
                    sp.dma_start(agu_sb[:, b], agu[bass.ds(e, 1)].rearrange("e p k g r -> (e p) k g r")).then_inc(agu_landed, 16)
                    sp.dma_start(bgu_sb[rows, b // HB], bgu[bass.ds(e, 1)].rearrange("e r f g m -> (e r) f g m")).then_inc(bgu_landed, 16)
                    sp.dma_start(adn_sb[:, b], adn[bass.ds(e, 1)].rearrange("e p f r -> (e p) f r")).then_inc(adn_landed, 16)
                    sp.dma_start(bdn_sb[rows, b // HB], bdn[bass.ds(e, 1)].rearrange("e r m -> (e r) m")).then_inc(bdn_landed, 16)

            load(0)
            with sp.Fori(1, NCH) as c:
                load(c)

        @block.gpsimd
        def _(pool):
            nc.gpsimd.memset(ident[:], 0.0).then_inc(consts_step, 1)
            nc.gpsimd.memset(lower[:], 1.0).then_inc(consts_step, 1)
            nc.gpsimd.memset(own[:], LORA_SCALE).then_inc(consts_step, 1)
            nc.gpsimd.iota(expert_no[:], [[1, E0]], base=0, channel_multiplier=0).then_inc(consts_done, 1)
            pool.wait_ge(consts_step, 3)
            nc.gpsimd.affine_select(out=ident[:], in_=ident[:], compare_op=ALU.not_equal, fill=1.0, base=0,
                                    pattern=[[-1, P]], channel_multiplier=1).then_inc(consts_done, 1)
            nc.gpsimd.affine_select(out=lower[:], in_=lower[:], compare_op=ALU.is_gt, fill=0.0, base=0,
                                    pattern=[[1, E0], [-1, E0]], channel_multiplier=0).then_inc(consts_done, 1)
            nc.gpsimd.affine_select(out=own[:], in_=own[:], compare_op=ALU.is_ge, fill=0.0, base=0,
                                    pattern=[[0, 2], [-R1, HB], [0, SEQ]], channel_multiplier=1).then_inc(consts_step, 1)
            pool.wait_ge(consts_step, 4)
            nc.gpsimd.affine_select(out=own[:], in_=own[:], compare_op=ALU.is_ge, fill=0.0, base=R1 - 1,
                                    pattern=[[0, 2], [R1, HB], [0, SEQ]], channel_multiplier=-1).then_inc(consts_done, 1)
            def store_x1(c):
                pool.wait_ge(x1_ready, KD * c + KD)
                pool.dma_start(x1_v[:, :, bass.ds(c * N, N)], x1_out[:]).then_inc(x1_stored, 16)

            store_x1(0)
            with pool.Fori(1, NCH) as c:
                store_x1(c)
            def store_out(c):
                pool.wait_ge(out_ready, KD * c + KD)
                pool.dma_start(out_v[:, :, bass.ds(c * N, N)], y_out[:]).then_inc(out_stored, 16)

            store_out(0)
            with pool.Fori(1, NCH) as c:
                store_out(c)
            pool.wait_ge(out_stored, 16 * NCH)

        @block.scalar
        def _(act):
            def layer0_chunk(c):
                act.wait_ge(h_ready, c + 1)
                after(act, hg_ready, c)
                nc.scalar.copy(h_sb[:], rot[:, 0, :]).then_inc(h_copied, 1)
                act.wait_ge(shifted, c + 1)
                nc.scalar.activation(ex[:], logit[:], ACT.Exp).then_inc(ex_ready, 1)

            layer0_chunk(0)
            with act.Fori(1, NCH) as c:
                layer0_chunk(c)
            def layer1_chunk(c):
                act.wait_ge(agu_landed, 16 * BPC * c + 16 * BPC)
                after(act, out_summed, c)
                nc.scalar.copy(agu_w[:].rearrange("p q b r -> p b q r"),
                               agu_sb[:].rearrange("p b k g r -> p b (k g) r")).then_inc(agu_packed, 1)
                act.wait_ge(adn_landed, 16 * BPC * c + 16 * BPC)
                nc.scalar.copy(adn_w[:].rearrange("p f b r -> p b f r"), adn_sb[:]).then_inc(adn_packed, 1)
                for f in range(NF):
                    act.wait_ge(gate_summed, NF * c + f + 1)
                    if f >= 2:
                        act.wait_ge(act_ready, NF * c + f - 1)
                    else:
                        after(act, act_ready, NF * c)
                    nc.scalar.activation(silu[:, f % 2], rot[:, (2 * f + 2) % 3, :], ACT.Silu).then_inc(silu_ready, 1)

            layer1_chunk(0)
            with act.Fori(1, NCH) as c:
                layer1_chunk(c)

        @block.vector
        def _(dve):
            G = 11
            dve.wait_ge(lang_in, 16 * (P // SEQ))
            dve.wait_ge(consts_done, 4)
            nc.vector.tensor_tensor(bias[:], lang_sb[:].unsqueeze(2).to_broadcast([P, NCH * SUB, E0]),
                                    expert_no[:].unsqueeze(1).to_broadcast([P, NCH * SUB, E0]),
                                    ALU.is_equal).then_inc(consts_step, 1)
            dve.wait_ge(consts_step, 5)
            nc.vector.tensor_scalar(bias[:], bias[:], LANG_BIAS, None, ALU.mult).then_inc(consts_step, 1)
            dve.wait_ge(consts_step, 6)
            def layer0_chunk(c):
                dve.wait_ge(x_landed, 16 * c + 16)
                after(dve, l0_ready, KD * c)
                after(dve, x1_ready, KD * c)
                nc.vector.tensor_copy(x_w[:], x_in[:]).then_inc(x_taken, 1)
                dve.wait_ge(logitT_ready, c + 1)
                nc.vector.tensor_copy(logitT[:], rot[0:E0, 1, :]).then_inc(logitT_copied, 1)
                dve.wait_ge(logit_ready, c + 1)
                nc.vector.tensor_tensor(logit[:], aux[:, 0:SUB * E0].rearrange("p (s e) -> p s e", s=SUB),
                                        bias[:, bass.ds(c * SUB, SUB), :], ALU.add).then_inc(gate_step, 1)
                dve.wait_ge(gate_step, G * c + 1)
                nc.vector.tensor_reduce(top[:], logit[:], AX_X, ALU.max).then_inc(gate_step, 1)
                dve.wait_ge(gate_step, G * c + 2)
                mine = logit[:].unsqueeze(3).to_broadcast([P, SUB, E0, E0])
                others = logit[:].unsqueeze(2).to_broadcast([P, SUB, E0, E0])
                nc.vector.tensor_tensor(above[:], others, mine, ALU.is_gt).then_inc(gate_step, 1)
                nc.vector.tensor_tensor(tied[:], others, mine, ALU.is_equal).then_inc(gate_step, 1)
                dve.wait_ge(gate_step, G * c + 4)
                nc.vector.tensor_tensor(logit[:], logit[:], top[:].unsqueeze(2).to_broadcast([P, SUB, E0]),
                                        ALU.subtract).then_inc(shifted, 1)
                nc.vector.tensor_tensor(tied[:], tied[:], lower[:].unsqueeze(1).to_broadcast([P, SUB, E0, E0]),
                                        ALU.mult).then_inc(gate_step, 1)
                dve.wait_ge(gate_step, G * c + 5)
                nc.vector.tensor_tensor(above[:], above[:], tied[:], ALU.add).then_inc(gate_step, 1)
                dve.wait_ge(gate_step, G * c + 6)
                nc.vector.tensor_reduce(rank[:], above[:], AX_X, ALU.add).then_inc(gate_step, 1)
                dve.wait_ge(gate_step, G * c + 7)
                dve.wait_ge(ex_ready, c + 1)
                nc.vector.scalar_tensor_tensor(out=ex[:], in0=rank[:], scalar=1.5, in1=ex[:], op0=ALU.is_lt,
                                               op1=ALU.mult).then_inc(gate_step, 1)
                dve.wait_ge(gate_step, G * c + 8)
                nc.vector.tensor_reduce(den[:], ex[:], AX_X, ALU.add).then_inc(gate_step, 1)
                dve.wait_ge(gate_step, G * c + 9)
                nc.vector.reciprocal(den[:], den[:]).then_inc(gate_step, 1)
                dve.wait_ge(gate_step, G * c + 10)
                nc.vector.tensor_tensor(ex[:], ex[:], den[:].unsqueeze(2).to_broadcast([P, SUB, E0]),
                                        ALU.mult).then_inc(gate_step, 1)
                dve.wait_ge(gate_step, G * c + 11)
                nc.vector.tensor_scalar(gate_rows[:], ex[:].unsqueeze(3).to_broadcast([P, SUB, E0, R0]),
                                        SCALING, None, ALU.mult).then_inc(gates_ready, 1)
                dve.wait_ge(gates_turned, c + 1)
                dve.wait_ge(h_copied, c + 1)
                nc.vector.tensor_tensor(hg_sb[:], h_sb[:], rot[:, 2, :], ALU.mult).then_inc(hg_ready, 1)
                after(dve, x1_stored, 16 * c)
                for m in range(KD):
                    dve.wait_ge(l0_ready, KD * c + m + 1)
                    nc.vector.tensor_tensor(x1_out[:, m], x_w[:, m], acc[:, m], ALU.add).then_inc(x1_ready, 1)

            layer0_chunk(0)
            with dve.Fori(1, NCH) as c:
                layer0_chunk(c)
            def layer1_chunk(c):
                dve.wait_ge(y_landed, 16 * c + 16)
                after(dve, out_ready, KD * c)
                after(dve, out_summed, c)
                nc.vector.tensor_copy(y_w[:], y_in[:]).then_inc(y_taken, 1)
                for g in range(2):
                    dve.wait_ge(tgu_summed, 2 * c + g + 1)
                    nc.vector.tensor_tensor(t_gu[:, g], rot[:, g, :], own[:].rearrange("p h b t -> p (h b t)"),
                                            ALU.mult).then_inc(tgu_ready, 1)
                for f in range(NF):
                    dve.wait_ge(silu_ready, NF * c + f + 1)
                    dve.wait_ge(up_summed, NF * c + f + 1)
                    if f >= 2:
                        dve.wait_ge(down_step, NF * c + f - 1)
                    nc.vector.tensor_tensor(act_sb[:, f % 2], silu[:, f % 2], rot[:, (2 * f + 3) % 3, :],
                                            ALU.mult).then_inc(act_ready, 1)
                dve.wait_ge(tdn_summed, c + 1)
                nc.vector.tensor_tensor(t_dn[:], aux[:], own[:].rearrange("p h b t -> p (h b t)"),
                                        ALU.mult).then_inc(tdn_ready, 1)
                after(dve, out_stored, 16 * c)
                dve.wait_ge(out_summed, c + 1)
                for m in range(KD):
                    nc.vector.tensor_tensor(y_out[:, m], y_w[:, m], acc[:, m], ALU.add).then_inc(out_ready, 1)

            layer1_chunk(0)
            with dve.Fori(1, NCH) as c:
                layer1_chunk(c)

        @block.tensor
        def _(pe):
            pe.wait_ge(weights0_in, 16 * 4)
            pe.wait_ge(consts_done, 4)
            def layer0_chunk(c):
                pe.wait_ge(x_taken, c + 1)
                after(pe, h_copied, c)
                for k in range(KD):
                    mm = nc.tensor.matmul(rot[:, 0, :], a0_sb[:, k], x_w[:, k], start=(k == 0), stop=(k == KD - 1))
                mm.then_inc(h_ready, 1)
                after(pe, logitT_copied, c)
                for k in range(KD):
                    mm = nc.tensor.matmul(rot[0:E0, 1, :], wr_sb[:, k], x_w[:, k], start=(k == 0), stop=(k == KD - 1))
                mm.then_inc(logitT_ready, 1)
                after(pe, x1_ready, KD * c)
                for m in range(KD):
                    for k in range(KD):
                        if m == 1 and k == KD - 1:
                            pe.wait_ge(logitT_copied, c + 1)
                        nc.tensor.matmul(acc[:, m], w0_sb[:, k, m * P:(m + 1) * P], x_w[:, k], start=(k == 0), stop=False)
                    if m == 1:
                        for s in range(SUB):
                            mm = nc.tensor.transpose(aux[:, E0 * s:E0 * (s + 1)], logitT[:, s * P:(s + 1) * P], ident[0:E0, 0:E0])
                        mm.then_inc(logit_ready, 1)
                    if m == KD - 1:
                        pe.wait_ge(gates_ready, c + 1)
                        for s in range(SUB):
                            mm = nc.tensor.transpose(rot[:, 2, s * P:(s + 1) * P], gate_rows[:, s].rearrange("p e r -> p (e r)"), ident[:])
                        mm.then_inc(gates_turned, 1)
                pe.wait_ge(hg_ready, c + 1)
                for m in range(KD):
                    nc.tensor.matmul(acc[:, m], b0_sb[:, m * P:(m + 1) * P], hg_sb[:], start=False, stop=True).then_inc(l0_ready, 1)

            layer0_chunk(0)
            with pe.Fori(1, NCH) as c:
                layer0_chunk(c)
            pe.wait_ge(x1_ready, KD * NCH)
            pe.wait_ge(weights1_in, 16 * NF)

            def down(c, f):
                pe.wait_ge(act_ready, NF * c + f + 1)
                a = act_sb[:, f % 2]
                for h in range(2):
                    tok = slice(h * HN, (h + 1) * HN)
                    mm = nc.tensor.matmul(aux[:, tok], adn_w[:, f, h * HB:(h + 1) * HB].rearrange("p b r -> p (b r)"), a[:, tok],
                                          start=(f == 0 and h == 0), stop=(f == NF - 1 and h == 1), skip_group_check=True)
                if f == NF - 1:
                    mm.then_inc(tdn_summed, 1)
                for m in range(KD):
                    mm = nc.tensor.matmul(acc[:, m], w1_sb[:, f, 2, m * P:(m + 1) * P], a, start=(f == 0), stop=False,
                                          skip_group_check=True)
                mm.then_inc(down_step, 1)

            def layer1_chunk(c):
                pe.wait_ge(y_taken, c + 1)
                pe.wait_ge(agu_packed, c + 1)
                after(pe, act_ready, NF * c)
                for g in range(2):
                    for h in range(2):
                        for k in range(KD):
                            mm = nc.tensor.matmul(rot[:, g, h * HN:(h + 1) * HN], agu_w[:, 2 * k + g, h * HB:(h + 1) * HB].rearrange("p b r -> p (b r)"),
                                                  y_w[:, k, h * HN:(h + 1) * HN], start=(k == 0), stop=(k == KD - 1))
                    mm.then_inc(tgu_summed, 1)
                for f in range(NF):
                    for g in range(2):
                        bank = rot[:, (2 * f + 2 + g) % 3, :]
                        if f == 0 and g == 1:
                            pe.wait_ge(tgu_ready, 2 * c + 1)
                        if f == 1 and g == 0:
                            pe.wait_ge(tgu_ready, 2 * c + 2)
                        if f >= 2 and g == 0:
                            pe.wait_ge(act_ready, NF * c + f - 1)
                        if f >= 1 and g == 1:
                            pe.wait_ge(silu_ready, NF * c + f)
                        for k in range(KD):
                            nc.tensor.matmul(bank, w1_sb[:, f, g, k * P:(k + 1) * P], y_w[:, k], start=(k == 0), stop=False,
                                             skip_group_check=True)
                        if f == 0:
                            pe.wait_ge(tgu_ready, 2 * c + g + 1)
                            pe.wait_ge(bgu_landed, 16 * BPC * c + 16 * BPC)
                        for h in range(2):
                            mm = nc.tensor.matmul(bank[:, h * HN:(h + 1) * HN], bgu_sb[:, h, f, g, :],
                                                  t_gu[:, g, h * HN:(h + 1) * HN], start=False, stop=(h == 1), skip_group_check=True)
                        mm.then_inc(up_summed if g else gate_summed, 1)
                    if f == 1:
                        pe.wait_ge(adn_packed, c + 1)
                        after(pe, tdn_ready, c)
                        after(pe, out_ready, KD * c)
                    if f >= 1:
                        down(c, f - 1)
                down(c, NF - 1)
                pe.wait_ge(tdn_ready, c + 1)
                pe.wait_ge(bdn_landed, 16 * BPC * c + 16 * BPC)
                for m in range(KD):
                    for h in range(2):
                        mm = nc.tensor.matmul(acc[:, m, h * HN:(h + 1) * HN], bdn_sb[:, h, m * P:(m + 1) * P],
                                              t_dn[:, h * HN:(h + 1) * HN], start=False, stop=(h == 1), skip_group_check=True)
                mm.then_inc(out_summed, 1)

            layer1_chunk(0)
            with pe.Fori(1, NCH) as c:
                layer1_chunk(c)


def kernel(x, itok_B_0_7, itok_B_2_6, L0_cond_W, L0_cond_Wr, L0_cond_A, L0_cond_B, L1_cond_W_gate, L1_cond_W_up,
           L1_cond_W_down, L1_cond_A_gate, L1_cond_B_gate, L1_cond_A_up, L1_cond_B_up, L1_cond_A_down, L1_cond_B_down):
    import numpy as np
    import concourse.bacc as bacc
    from concourse.bass_utils import run_bass_kernel_spmd

    def rows_to_partitions(w):
        return np.ascontiguousarray(np.asarray(w).reshape(-1, P, w.shape[-1]).transpose(1, 0, 2))

    def padded(w, axis):
        w = np.asarray(w)
        pad = [(0, 0)] * w.ndim
        pad[axis] = (0, FP - F)
        return np.pad(w, pad)

    def hidden_out(w):
        return padded(w, 0).reshape(NF, P, KD, P).transpose(0, 3, 2, 1).reshape(NF, P, D)

    x = np.asarray(x)
    w1 = np.stack([hidden_out(L1_cond_W_gate), hidden_out(L1_cond_W_up),
                   padded(L1_cond_W_down, 1).T.reshape(NF, P, D)], axis=2)
    a_gu = np.stack([np.asarray(L1_cond_A_gate)[0], np.asarray(L1_cond_A_up)[0]])
    agu = a_gu.reshape(2, E1, R1, KD, P).transpose(1, 4, 3, 0, 2)
    b_gu = np.stack([padded(np.asarray(L1_cond_B_gate)[0], 1), padded(np.asarray(L1_cond_B_up)[0], 1)])
    bgu = b_gu.reshape(2, E1, NF, P, R1).transpose(1, 4, 2, 0, 3)
    adn = padded(np.asarray(L1_cond_A_down)[0], 2).reshape(E1, R1, NF, P).transpose(0, 3, 2, 1)
    bdn = np.asarray(L1_cond_B_down)[0].transpose(0, 2, 1)
    inputs = {
        "xT": x.reshape(TOK, D).T,
        "lang": np.asarray(itok_B_0_7).reshape(NCH * SUB, P // SEQ).T,
        "adapter": np.asarray(itok_B_2_6).reshape(1, BATCH),
        "w0": rows_to_partitions(np.asarray(L0_cond_W).T),
        "a0": rows_to_partitions(np.asarray(L0_cond_A).reshape(E0 * R0, D).T),
        "b0": np.asarray(L0_cond_B).transpose(0, 2, 1).reshape(E0 * R0, D),
        "wr": rows_to_partitions(np.asarray(L0_cond_Wr).T),
        "w1": w1, "agu": agu, "bgu": bgu, "adn": adn, "bdn": bdn,
    }
    inputs = {n: np.ascontiguousarray(a) for n, a in inputs.items()}
    nc = bacc.Bacc("TRN2", target_bir_lowering=False, num_devices=1)
    aps = [nc.dram_tensor(n, a.shape, mybir.dt.from_np(a.dtype), kind="ExternalInput").ap() for n, a in inputs.items()]
    out = nc.dram_tensor("outT", (D, TOK), F32, kind="ExternalOutput").ap()
    build(nc, *aps, out)
    r = run_bass_kernel_spmd(nc, [inputs], core_ids=[0])
    return np.ascontiguousarray(r.results[0]["outT"].T).reshape(BATCH, SEQ, D)
```

```python
from contextlib import ExitStack

import concourse.bass as bass
from concourse import mybir

ALU = mybir.AluOpType
ACT = mybir.ActivationFunctionType
AX_X = mybir.AxisListType.X
F32 = mybir.dt.float32
F32R = mybir.dt.float32r
I32 = mybir.dt.int32

P = 128
BATCH, SEQ, D = 128, 32, 512
TOK = BATCH * SEQ
E0, R0 = 8, 16
E1, R1 = 16, 16
F = 1376
NF = -(-F // P)
FP = NF * P
KD = D // P
N = 512
NCH = TOK // N
SUB = N // P
BPC = N // SEQ
HB = BPC // 2
HN = N // 2
GROUP = 3
NG = -(-NF // GROUP)
TILE_W = 2 * D + D
LANG_BIAS, SCALING, LORA_SCALE = 5.0, 2.0, 0.5


def build(nc, xT, lang, adapter, w0, a0, b0, wr, w1, agu, bgu, adn, bdn, outT):
    x1_dram = nc.dram_tensor("x1_scratch", (D, TOK), F32, kind="Internal").ap()
    x_v = xT.rearrange("(k p) t -> p k t", p=P)
    x1_v = x1_dram.rearrange("(k p) t -> p k t", p=P)
    out_v = outT.rearrange("(k p) t -> p k t", p=P)

    def after(eng, semaphore, n):
        if not isinstance(n, int) or n > 0:
            eng.wait_ge(semaphore, n)

    with ExitStack() as ctx:
        def sb(name, shape, dt=F32, where=ctx):
            return where.enter_context(nc.sbuf_tensor(name, shape, dt))

        def pair(name, shape, where=ctx):
            return sb(name + "_hi", shape, F32R, where), sb(name + "_lo", shape, F32R, where)

        def sem(name):
            return ctx.enter_context(nc.semaphore(name))

        w1_sb = sb("w1_sb", [P, NF, TILE_W])
        agu_sb = sb("agu_sb", [P, BPC, KD * 2, R1])
        bgu_sb = sb("bgu_sb", [P, 2, 2, GROUP, 2, P])
        adn_sb = sb("adn_sb", [P, BPC, NF, R1])
        bdn_sb = sb("bdn_sb", [P, 2, D])
        own = sb("own", [P, HB * SEQ])
        adapter_sb = sb("adapter_sb", [1, BATCH], I32)
        x_in0 = sb("x_in0", [P, KD, N])
        x_hi, x_lo = pair("x", [P, KD, N])
        y_out = sb("y_out", [P, KD, N])

        only0 = ExitStack()
        x_in = [x_in0, sb("x_in1", [P, KD, N], where=only0)]
        w0_sb = sb("w0_sb", [P, KD, D], where=only0)
        a0_sb = sb("a0_sb", [P, KD, P], where=only0)
        b0_sb = sb("b0_sb", [P, D], where=only0)
        wr_sb = sb("wr_sb", [P, KD, E0], where=only0)
        w0_hi, w0_lo = pair("w0", [P, KD, D], only0)
        a0_hi, a0_lo = pair("a0", [P, KD, P], only0)
        b0_hi, b0_lo = pair("b0", [P, D], only0)
        h_sb = sb("h_sb", [P, N], where=only0)
        hg_sb = sb("hg_sb", [P, N], where=only0)
        hg_hi, hg_lo = pair("hg", [P, N], only0)
        logitT = sb("logitT", [E0, N], where=only0)
        ident = sb("ident", [P, P], where=only0)
        lower = sb("lower", [P, E0, E0], where=only0)
        lang_sb = sb("lang_sb", [P, NCH * SUB], I32, only0)
        expert_no = sb("expert_no", [P, E0], I32, only0)
        bias = sb("bias", [P, NCH * SUB, E0], where=only0)
        logit = sb("logit", [P, SUB, E0], where=only0)
        top = sb("top", [P, SUB], where=only0)
        ex = sb("ex", [P, SUB, E0], where=only0)
        above = sb("above", [P, SUB, E0, E0], where=only0)
        tied = sb("tied", [P, SUB, E0, E0], where=only0)
        rank = sb("rank", [P, SUB, E0], where=only0)
        den = sb("den", [P, SUB], where=only0)
        gate_rows = sb("gate_rows", [P, SUB, E0, R0], where=only0)
        only0.close()

        gu_hi, gu_lo = pair("gu", [P, 2, 3 * D])
        dn_hi, dn_lo = pair("dn", [P, 2, D + BPC * R1])
        bd_hi, bd_lo = pair("bd", [P, 2, D])
        t_sb = sb("t_sb", [P, 2, N])
        t_hi, t_lo = pair("t", [P, 2, N])
        silu = sb("silu", [P, 2, N])
        h1_hi, h1_lo = pair("h1", [P, 2, N])

        acc = ctx.enter_context(nc.psum_tensor("acc", [P, KD, N], F32))
        rot = ctx.enter_context(nc.psum_tensor("rot", [P, 3, N], F32))
        aux = ctx.enter_context(nc.psum_tensor("aux", [P, N], F32))

        small0_landed, w0_landed, lang_landed = sem("small0_landed"), sem("w0_landed"), sem("lang_landed")
        w1_landed, adapter_landed = sem("w1_landed"), sem("adapter_landed")
        consts_step, consts_done = sem("consts_step"), sem("consts_done")
        w0_hi_done, w0_lo_done = sem("w0_hi_done"), sem("w0_lo_done")
        x_landed = [sem("x_landed0"), sem("x_landed1")]
        x_hi_done, x_lo_done = sem("x_hi_done"), sem("x_lo_done")
        h_summed, h_copied = sem("h_summed"), sem("h_copied")
        logitT_summed, logitT_copied, logit_turned = sem("logitT_summed"), sem("logitT_copied"), sem("logit_turned")
        gate_step, shifted, ex_done = sem("gate_step"), sem("shifted"), sem("ex_done")
        gates_done, gates_turned = sem("gates_done"), sem("gates_turned")
        hg_done, hg_hi_done, hg_lo_done = sem("hg_done"), sem("hg_hi_done"), sem("hg_lo_done")
        base_summed, l0_summed, x1_ready, x1_stored = sem("base_summed"), sem("l0_summed"), sem("x1_ready"), sem("x1_stored")
        y_landed, res_landed = sem("y_landed"), sem("res_landed")
        y_hi_done, y_lo_done = sem("y_hi_done"), sem("y_lo_done")
        agu_landed, adn_landed, bdn_landed = sem("agu_landed"), sem("adn_landed"), sem("bdn_landed")
        bgu_landed = [sem("bgu_landed0"), sem("bgu_landed1")]
        gu_hi_done, gu_lo_done = sem("gu_hi_done"), sem("gu_lo_done")
        dn_hi_done, dn_lo_done = sem("dn_hi_done"), sem("dn_lo_done")
        bd_hi_done, bd_lo_done = sem("bd_hi_done"), sem("bd_lo_done")
        tgu_summed, tdn_summed = sem("tgu_summed"), sem("tdn_summed")
        t_done, t_hi_done, t_lo_done = sem("t_done"), sem("t_hi_done"), sem("t_lo_done")
        gate_summed, up_summed, silu_done = sem("gate_summed"), sem("up_summed"), sem("silu_done")
        h1_done, h1_hi_done, h1_lo_done = sem("h1_done"), sem("h1_hi_done"), sem("h1_lo_done")
        down_summed, out_summed, out_ready, out_stored = sem("down_summed"), sem("out_summed"), sem("out_ready"), sem("out_stored")
        ALL = 16 * BPC
        W = NF + 1
        T = 3

        block = ctx.enter_context(nc.Block())

        @block.sync
        def _(sp):
            def load_x(c, slot):
                sp.dma_start(x_in[slot][:], x_v[:, :, bass.ds(c * N, N)]).then_inc(x_landed[slot], 16)

            def adapters(c):
                return [sp.value_load(adapter_sb[0:1, bass.ds(c * BPC + b, 1)], min_val=0, max_val=E1 - 1) for b in range(BPC)]

            def rows(b):
                return slice(R1 * (b % HB), R1 * (b % HB + 1))

            def gather_agu(named):
                for b, e in enumerate(named):
                    sp.dma_start(agu_sb[:, b], agu[bass.ds(e, 1)].rearrange("e p q r -> (e p) q r")).then_inc(agu_landed, 16)

            def gather_adn(named):
                for b, e in enumerate(named):
                    sp.dma_start(adn_sb[:, b], adn[bass.ds(e, 1)].rearrange("e p f r -> (e p) f r")).then_inc(adn_landed, 16)

            def gather_bdn(named):
                for b, e in enumerate(named):
                    sp.dma_start(bdn_sb[rows(b), b // HB], bdn[bass.ds(e, 1)].rearrange("e r m -> (e r) m")).then_inc(bdn_landed, 16)

            def gather_bgu(named, q):
                f0, n = q * GROUP, min(GROUP, NF - q * GROUP)
                for b, e in enumerate(named):
                    src = bgu[bass.ds(e, 1), :, f0:f0 + n].rearrange("e r f g m -> (e r) f g m")
                    sp.dma_start(bgu_sb[rows(b), q % 2, b // HB, 0:n], src).then_inc(bgu_landed[q % 2], 16)

            load_x(0, 0)
            sp.dma_start(wr_sb[:], wr).then_inc(small0_landed, 16)
            sp.dma_start(a0_sb[:], a0).then_inc(small0_landed, 16)
            sp.dma_start(w0_sb[:], w0).then_inc(w0_landed, 16)
            for j in range(P // SEQ):
                sp.dma_start(lang_sb[SEQ * j:SEQ * (j + 1), :],
                             lang[j:j + 1].to_broadcast([SEQ, NCH * SUB])).then_inc(lang_landed, 16)
            sp.dma_start(b0_sb[:], b0).then_inc(w0_landed, 16)
            load_x(1, 1)
            sp.dma_start(adapter_sb[:], adapter).then_inc(adapter_landed, 16)
            sp.wait_ge(adapter_landed, 16)
            first = adapters(0)
            early = [lambda: gather_agu(first), lambda: gather_bgu(first, 0), lambda: gather_adn(first),
                     lambda: gather_bgu(first, 1), lambda: gather_bdn(first), lambda: None]
            for c in range(2, NCH):
                sp.wait_ge(x1_ready, KD * (c - 1))
                load_x(c, c % 2)
                early[c - 2]()

            def layer1_chunk(c, last=False):
                named = adapters(c)
                after(sp, out_stored, 16 * c)
                sp.dma_start(y_out[:], x1_v[:, :, bass.ds(c * N, N)]).then_inc(res_landed, 16)
                if not last:
                    sp.wait_ge(y_lo_done, KD * c + KD)
                    sp.dma_start(x_in0[:], x1_v[:, :, bass.ds(c * N + N, N)]).then_inc(y_landed, 16)
                sp.wait_ge(gu_lo_done, W * c + 1 + 1 * GROUP)
                gather_bgu(named, 2)
                sp.wait_ge(gu_lo_done, W * c + 1 + 2 * GROUP)
                gather_bgu(named, 3)
                if not last:
                    named = adapters(c + 1)
                    sp.wait_ge(dn_lo_done, W * c + 1)
                    gather_agu(named)
                    sp.wait_ge(gu_lo_done, W * c + 1 + 3 * GROUP)
                    gather_bgu(named, 0)
                    sp.wait_ge(gu_lo_done, W * c + W)
                    gather_bgu(named, 1)
                    sp.wait_ge(dn_lo_done, W * c + W)
                    gather_adn(named)
                    sp.wait_ge(bd_lo_done, c + 1)
                    gather_bdn(named)

            sp.wait_ge(x1_stored, 16 * (NCH - 1))
            sp.dma_start(x_in0[:], x1_v[:, :, 0:N]).then_inc(y_landed, 16)
            sp.wait_ge(x1_stored, 16 * NCH)
            layer1_chunk(0)
            with sp.Fori(1, NCH - 1) as c:
                layer1_chunk(c)
            layer1_chunk(NCH - 1, last=True)

        @block.gpsimd
        def _(pool):
            nc.gpsimd.memset(ident[:], 0.0).then_inc(consts_step, 1)
            nc.gpsimd.memset(lower[:], 1.0).then_inc(consts_step, 1)
            nc.gpsimd.memset(own[:], LORA_SCALE).then_inc(consts_step, 1)
            nc.gpsimd.iota(expert_no[:], [[1, E0]], base=0, channel_multiplier=0).then_inc(consts_done, 1)
            pool.wait_ge(consts_step, 3)
            nc.gpsimd.affine_select(out=ident[:], in_=ident[:], compare_op=ALU.not_equal, fill=1.0, base=0,
                                    pattern=[[-1, P]], channel_multiplier=1).then_inc(consts_done, 1)
            nc.gpsimd.affine_select(out=lower[:], in_=lower[:], compare_op=ALU.is_gt, fill=0.0, base=0,
                                    pattern=[[1, E0], [-1, E0]], channel_multiplier=0).then_inc(consts_done, 1)
            for f in range(NF):
                pool.dma_start(w1_sb[:, f], w1[f]).then_inc(w1_landed, 16)
            nc.gpsimd.affine_select(out=own[:], in_=own[:], compare_op=ALU.is_ge, fill=0.0, base=0,
                                    pattern=[[-R1, HB], [0, SEQ]], channel_multiplier=1).then_inc(consts_step, 1)
            pool.wait_ge(consts_step, 4)
            nc.gpsimd.affine_select(out=own[:], in_=own[:], compare_op=ALU.is_ge, fill=0.0, base=R1 - 1,
                                    pattern=[[R1, HB], [0, SEQ]], channel_multiplier=-1).then_inc(consts_done, 1)
            with pool.Fori(0, NCH) as c:
                pool.wait_ge(x1_ready, KD * c + KD)
                pool.dma_start(x1_v[:, :, bass.ds(c * N, N)], y_out[:]).then_inc(x1_stored, 16)
            with pool.Fori(0, NCH) as c:
                pool.wait_ge(out_ready, KD * c + KD)
                pool.dma_start(out_v[:, :, bass.ds(c * N, N)], y_out[:]).then_inc(out_stored, 16)
            pool.wait_ge(out_stored, 16 * NCH)

        def agu_parts():
            src = agu_sb[:].rearrange("p b q r -> p q b r")
            in_gu, in_dn = 3 * D // (BPC * R1), 2
            first = [x[:, 0, :].rearrange("p (q b r) -> p q b r", q=in_gu, b=BPC) for x in (gu_hi, gu_lo)]
            rest = [x[:, 0, 0:D].rearrange("p (q b r) -> p q b r", q=in_dn, b=BPC) for x in (dn_hi, dn_lo)]
            return (src[:, 0:in_gu], *first), (src[:, in_gu:], *rest)

        def gu_parts(f):
            s = (f + 1) % 2
            b = bgu_sb[:, (f // GROUP) % 2, :, f % GROUP].rearrange("p h g m -> p h (g m)")
            return ((w1_sb[:, f, 0:2 * D], gu_hi[:, s, 0:2 * D], gu_lo[:, s, 0:2 * D]),
                    (b, *[x[:, s, 2 * D:].rearrange("p (h m) -> p h m", h=2) for x in (gu_hi, gu_lo)]))

        def dn_parts(f):
            s = (f + 1) % 2
            return ((w1_sb[:, f, 2 * D:], dn_hi[:, s, 0:D], dn_lo[:, s, 0:D]),
                    (adn_sb[:, :, f], *[x[:, s, D:].rearrange("p (b r) -> p b r", b=BPC) for x in (dn_hi, dn_lo)]))

        def bgu_arrived(eng, c, f):
            q = f // GROUP
            eng.wait_ge(bgu_landed[q % 2], ALL * (2 * c + q // 2 + 1))

        @block.scalar
        def _(act):
            def his(parts, done):
                for src, hi, _ in parts:
                    ins = nc.scalar.copy(hi, src)
                ins.then_inc(done, 1)

            act.wait_ge(x_landed[0], 16)
            for k in range(KD):
                nc.scalar.copy(x_hi[:, k], x_in0[:, k]).then_inc(x_hi_done, 1)
            act.wait_ge(small0_landed, 32)
            nc.scalar.copy(a0_hi[:], a0_sb[:]).then_inc(w0_hi_done, 1)
            act.wait_ge(w0_landed, 32)
            nc.scalar.copy(w0_hi[:], w0_sb[:]).then_inc(w0_hi_done, 1)
            nc.scalar.copy(b0_hi[:], b0_sb[:]).then_inc(w0_hi_done, 1)
            act.wait_ge(logitT_summed, 1)
            nc.scalar.copy(logitT[:], rot[0:E0, 1, :]).then_inc(logitT_copied, 1)

            def layer0_chunk(i, j, last=False):
                c, slot, turn = 2 * i + j, (j + 1) % 2, i + (j + 1) // 2
                act.wait_ge(h_summed, c + 1)
                after(act, hg_done, c)
                nc.scalar.copy(h_sb[:], rot[:, 0, :]).then_inc(h_copied, 1)
                act.wait_ge(shifted, c + 1)
                nc.scalar.activation(ex[:], logit[:], ACT.Exp).then_inc(ex_done, 1)
                act.wait_ge(hg_done, c + 1)
                nc.scalar.copy(hg_hi[:], hg_sb[:]).then_inc(hg_hi_done, 1)
                if not last:
                    act.wait_ge(x_landed[slot], 16 * turn + 16)
                    act.wait_ge(base_summed, c + 1)
                    for k in range(KD):
                        nc.scalar.copy(x_hi[:, k], x_in[slot][:, k]).then_inc(x_hi_done, 1)
                    act.wait_ge(logitT_summed, c + 2)
                    nc.scalar.copy(logitT[:], rot[0:E0, 1, :]).then_inc(logitT_copied, 1)

            layer0_chunk(0, 0)
            layer0_chunk(0, 1)
            with act.Fori(1, NCH // 2 - 1) as i:
                layer0_chunk(i, 0)
                layer0_chunk(i, 1)
            layer0_chunk(NCH // 2 - 1, 0)
            layer0_chunk(NCH // 2 - 1, 1, last=True)

            def y_his(c):
                act.wait_ge(y_landed, 16 * c + 16)
                for k in range(KD):
                    nc.scalar.copy(x_hi[:, k], x_in0[:, k]).then_inc(y_hi_done, 1)

            act.wait_ge(base_summed, NCH)
            y_his(0)
            act.wait_ge(x1_ready, KD * NCH)
            act.wait_ge(agu_landed, ALL)
            for part in agu_parts():
                his([part], gu_hi_done if part[1].shape[1] > 2 else dn_hi_done)
            act.wait_ge(w1_landed, 16 * NF)
            bgu_arrived(act, 0, 0)
            his(gu_parts(0), gu_hi_done)

            def layer1_chunk(c, last=False):
                for g in range(2):
                    act.wait_ge(t_done, T * c + g + 1)
                    nc.scalar.copy(t_hi[:, g], t_sb[:, g]).then_inc(t_hi_done, 1)
                bgu_arrived(act, c, 1)
                his(gu_parts(1), gu_hi_done)
                for f in range(NF):
                    act.wait_ge(gate_summed, NF * c + f + 1)
                    if f >= 2:
                        act.wait_ge(h1_lo_done, NF * c + f - 1)
                    else:
                        after(act, h1_lo_done, NF * c)
                    nc.scalar.activation(silu[:, f % 2], rot[:, (2 * f + 2) % 3, :], ACT.Silu).then_inc(silu_done, 1)
                    act.wait_ge(h1_done, NF * c + f + 1)
                    if f >= 2:
                        act.wait_ge(down_summed, NF * c + f - 1)
                    else:
                        after(act, down_summed, NF * c)
                    nc.scalar.copy(h1_hi[:, f % 2], silu[:, f % 2]).then_inc(h1_hi_done, 1)
                    if f == 0:
                        after(act, down_summed, NF * c)
                        act.wait_ge(adn_landed, ALL * c + ALL)
                        his(dn_parts(0), dn_hi_done)
                    if f + 2 < NF:
                        bgu_arrived(act, c, f + 2)
                        his(gu_parts(f + 2), gu_hi_done)
                    if f == 8:
                        act.wait_ge(bdn_landed, ALL * c + ALL)
                        after(act, out_summed, KD * c)
                        nc.scalar.copy(bd_hi[:], bdn_sb[:]).then_inc(bd_hi_done, 1)
                    if f == NF - 2 and not last:
                        act.wait_ge(agu_landed, ALL * c + 2 * ALL)
                        his([agu_parts()[0]], gu_hi_done)
                    if f < NF - 1:
                        if f >= 1:
                            act.wait_ge(down_summed, NF * c + f)
                        his(dn_parts(f + 1), dn_hi_done)
                if not last:
                    y_his(c + 1)
                    act.wait_ge(down_summed, NF * c + NF - 1)
                    his([agu_parts()[1]], dn_hi_done)
                act.wait_ge(t_done, T * c + 3)
                nc.scalar.copy(t_hi[:, 0], t_sb[:, 0]).then_inc(t_hi_done, 1)
                if not last:
                    bgu_arrived(act, c + 1, 0)
                    his(gu_parts(0), gu_hi_done)

            layer1_chunk(0)
            with act.Fori(1, NCH - 1) as c:
                layer1_chunk(c)
            layer1_chunk(NCH - 1, last=True)

        @block.vector
        def _(dve):
            G = 11

            def lo(out, x, hi, done):
                nc.vector.tensor_tensor(out, x, hi.bitcast(F32), ALU.subtract).then_inc(done, 1)

            def los(parts, done):
                for src, hi, low in parts:
                    ins = nc.vector.tensor_tensor(low, src, hi.bitcast(F32), ALU.subtract)
                ins.then_inc(done, 1)

            for k in range(KD):
                dve.wait_ge(x_hi_done, k + 1)
                lo(x_lo[:, k], x_in0[:, k], x_hi[:, k], x_lo_done)
            dve.wait_ge(lang_landed, 16 * (P // SEQ))
            dve.wait_ge(consts_done, 3)
            nc.vector.tensor_tensor(bias[:], lang_sb[:].unsqueeze(2).to_broadcast([P, NCH * SUB, E0]),
                                    expert_no[:].unsqueeze(1).to_broadcast([P, NCH * SUB, E0]),
                                    ALU.is_equal).then_inc(gate_step, 1)
            for n, (low, x, hi) in enumerate([(a0_lo, a0_sb, a0_hi), (w0_lo, w0_sb, w0_hi), (b0_lo, b0_sb, b0_hi)]):
                dve.wait_ge(w0_hi_done, n + 1)
                lo(low[:], x[:], hi[:], w0_lo_done)
            dve.wait_ge(gate_step, 1)
            nc.vector.tensor_scalar(bias[:], bias[:], LANG_BIAS, None, ALU.mult).then_inc(gate_step, 1)

            def layer0_chunk(i, j, last=False):
                c, slot = 2 * i + j, (j + 1) % 2
                g0 = G * c + 2
                dve.wait_ge(gate_step, g0)
                dve.wait_ge(logit_turned, c + 1)
                nc.vector.tensor_tensor(logit[:], aux[:, 0:SUB * E0].rearrange("p (s e) -> p s e", s=SUB),
                                        bias[:, bass.ds(c * SUB, SUB), :], ALU.add).then_inc(gate_step, 1)
                dve.wait_ge(gate_step, g0 + 1)
                nc.vector.tensor_reduce(top[:], logit[:], AX_X, ALU.max).then_inc(gate_step, 1)
                mine = logit[:].unsqueeze(3).to_broadcast([P, SUB, E0, E0])
                others = logit[:].unsqueeze(2).to_broadcast([P, SUB, E0, E0])
                nc.vector.tensor_tensor(above[:], others, mine, ALU.is_gt).then_inc(gate_step, 1)
                nc.vector.tensor_tensor(tied[:], others, mine, ALU.is_equal).then_inc(gate_step, 1)
                dve.wait_ge(gate_step, g0 + 4)
                nc.vector.tensor_tensor(logit[:], logit[:], top[:].unsqueeze(2).to_broadcast([P, SUB, E0]),
                                        ALU.subtract).then_inc(shifted, 1)
                nc.vector.tensor_tensor(tied[:], tied[:], lower[:].unsqueeze(1).to_broadcast([P, SUB, E0, E0]),
                                        ALU.mult).then_inc(gate_step, 1)
                dve.wait_ge(gate_step, g0 + 5)
                nc.vector.tensor_tensor(above[:], above[:], tied[:], ALU.add).then_inc(gate_step, 1)
                dve.wait_ge(gate_step, g0 + 6)
                nc.vector.tensor_reduce(rank[:], above[:], AX_X, ALU.add).then_inc(gate_step, 1)
                dve.wait_ge(gate_step, g0 + 7)
                dve.wait_ge(ex_done, c + 1)
                nc.vector.scalar_tensor_tensor(out=ex[:], in0=rank[:], scalar=1.5, in1=ex[:], op0=ALU.is_lt,
                                               op1=ALU.mult).then_inc(gate_step, 1)
                dve.wait_ge(gate_step, g0 + 8)
                nc.vector.tensor_reduce(den[:], ex[:], AX_X, ALU.add).then_inc(gate_step, 1)
                dve.wait_ge(gate_step, g0 + 9)
                nc.vector.reciprocal(den[:], den[:]).then_inc(gate_step, 1)
                dve.wait_ge(gate_step, g0 + 10)
                nc.vector.tensor_tensor(ex[:], ex[:], den[:].unsqueeze(2).to_broadcast([P, SUB, E0]),
                                        ALU.mult).then_inc(gate_step, 1)
                dve.wait_ge(gate_step, g0 + 11)
                nc.vector.tensor_scalar(gate_rows[:], ex[:].unsqueeze(3).to_broadcast([P, SUB, E0, R0]),
                                        SCALING, None, ALU.mult).then_inc(gates_done, 1)
                dve.wait_ge(gates_turned, c + 1)
                dve.wait_ge(h_copied, c + 1)
                nc.vector.tensor_tensor(hg_sb[:], h_sb[:], rot[:, 2, :], ALU.mult).then_inc(hg_done, 1)
                dve.wait_ge(hg_hi_done, c + 1)
                lo(hg_lo[:], hg_sb[:], hg_hi[:], hg_lo_done)
                if not last:
                    for k in range(KD):
                        dve.wait_ge(x_hi_done, KD * c + KD + k + 1)
                        lo(x_lo[:, k], x_in[slot][:, k], x_hi[:, k], x_lo_done)
                after(dve, x1_stored, 16 * c)
                for m in range(KD):
                    dve.wait_ge(l0_summed, KD * c + m + 1)
                    nc.vector.tensor_tensor(y_out[:, m], x_in[j][:, m], acc[:, m], ALU.add).then_inc(x1_ready, 1)

            layer0_chunk(0, 0)
            layer0_chunk(0, 1)
            with dve.Fori(1, NCH // 2 - 1) as i:
                layer0_chunk(i, 0)
                layer0_chunk(i, 1)
            layer0_chunk(NCH // 2 - 1, 0)
            layer0_chunk(NCH // 2 - 1, 1, last=True)

            def y_los(c):
                for k in range(KD):
                    dve.wait_ge(y_hi_done, KD * c + k + 1)
                    lo(x_lo[:, k], x_in0[:, k], x_hi[:, k], y_lo_done)

            y_los(0)
            dve.wait_ge(gu_hi_done, 1)
            los([agu_parts()[0]], gu_lo_done)
            dve.wait_ge(dn_hi_done, 1)
            los([agu_parts()[1]], dn_lo_done)
            dve.wait_ge(gu_hi_done, 2)
            los(gu_parts(0), gu_lo_done)
            dve.wait_ge(consts_done, 4)
            halves = own[:].unsqueeze(1).to_broadcast([P, 2, HN])

            def layer1_chunk(c, last=False):
                for g in range(2):
                    dve.wait_ge(tgu_summed, 2 * c + g + 1)
                    nc.vector.tensor_tensor(t_sb[:, g].rearrange("p (h t) -> p h t", h=2),
                                            rot[:, g, :].rearrange("p (h t) -> p h t", h=2), halves,
                                            ALU.mult).then_inc(t_done, 1)
                for g in range(2):
                    dve.wait_ge(t_hi_done, T * c + g + 1)
                    lo(t_lo[:, g], t_sb[:, g], t_hi[:, g], t_lo_done)
                dve.wait_ge(gu_hi_done, W * c + 3)
                los(gu_parts(1), gu_lo_done)
                for f in range(NF):
                    s = silu[:, f % 2]
                    dve.wait_ge(silu_done, NF * c + f + 1)
                    dve.wait_ge(up_summed, NF * c + f + 1)
                    nc.vector.tensor_tensor(s, s, rot[:, (2 * f + 3) % 3, :], ALU.mult).then_inc(h1_done, 1)
                    dve.wait_ge(h1_hi_done, NF * c + f + 1)
                    lo(h1_lo[:, f % 2], s, h1_hi[:, f % 2], h1_lo_done)
                    if f == 0:
                        dve.wait_ge(dn_hi_done, W * c + 2)
                        los(dn_parts(0), dn_lo_done)
                    if f + 2 < NF:
                        dve.wait_ge(gu_hi_done, W * c + f + 4)
                        los(gu_parts(f + 2), gu_lo_done)
                    if f == 8:
                        dve.wait_ge(bd_hi_done, c + 1)
                        lo(bd_lo[:], bdn_sb[:], bd_hi[:], bd_lo_done)
                    if f == NF - 2 and not last:
                        dve.wait_ge(gu_hi_done, W * c + W + 1)
                        los([agu_parts()[0]], gu_lo_done)
                    if f < NF - 1:
                        dve.wait_ge(dn_hi_done, W * c + f + 3)
                        los(dn_parts(f + 1), dn_lo_done)
                if not last:
                    y_los(c + 1)
                    dve.wait_ge(dn_hi_done, W * c + W + 1)
                    los([agu_parts()[1]], dn_lo_done)
                dve.wait_ge(tdn_summed, c + 1)
                nc.vector.tensor_tensor(t_sb[:, 0].rearrange("p (h t) -> p h t", h=2),
                                        aux[:].rearrange("p (h t) -> p h t", h=2), halves,
                                        ALU.mult).then_inc(t_done, 1)
                dve.wait_ge(t_hi_done, T * c + 3)
                lo(t_lo[:, 0], t_sb[:, 0], t_hi[:, 0], t_lo_done)
                if not last:
                    dve.wait_ge(gu_hi_done, W * c + W + 2)
                    los(gu_parts(0), gu_lo_done)
                dve.wait_ge(res_landed, 16 * c + 16)
                for m in range(KD):
                    dve.wait_ge(out_summed, KD * c + m + 1)
                    nc.vector.tensor_tensor(y_out[:, m], y_out[:, m], acc[:, m], ALU.add).then_inc(out_ready, 1)

            layer1_chunk(0)
            with dve.Fori(1, NCH - 1) as c:
                layer1_chunk(c)
            layer1_chunk(NCH - 1, last=True)

        @block.tensor
        def _(pe):
            def product(out, w, x, first, last):
                (wh, wl), (xh, xl) = w, x
                nc.tensor.matmul(out, wh, xh, start=first, stop=False, skip_group_check=True)
                nc.tensor.matmul(out, wh, xl, start=False, stop=False, skip_group_check=True)
                return nc.tensor.matmul(out, wl, xh, start=False, stop=last, skip_group_check=True)

            def both(operand, *index):
                return tuple(x[(slice(None), *index)] for x in operand)

            X = (x_hi, x_lo)

            def router(slot, turn):
                pe.wait_ge(x_landed[slot], 16 * turn + 16)
                for k in range(KD):
                    mm = nc.tensor.matmul(rot[0:E0, 1, :], wr_sb[:, k], x_in[slot][:, k], start=(k == 0), stop=(k == KD - 1))
                mm.then_inc(logitT_summed, 1)

            pe.wait_ge(small0_landed, 32)
            router(0, 0)
            pe.wait_ge(consts_done, 3)

            def layer0_chunk(i, j, last=False):
                c, slot, turn = 2 * i + j, (j + 1) % 2, i + (j + 1) // 2
                pe.wait_ge(x_lo_done, KD * c + KD)
                pe.wait_ge(w0_lo_done, 1)
                for k in range(KD):
                    if k == 1:
                        pe.wait_ge(logitT_copied, c + 1)
                    mm = product(rot[:, 0, :], both((a0_hi, a0_lo), k), both(X, k), k == 0, k == KD - 1)
                    if k == 1:
                        for s in range(SUB):
                            turned = nc.tensor.transpose(aux[:, E0 * s:E0 * (s + 1)], logitT[:, s * P:(s + 1) * P], ident[0:E0, 0:E0])
                        turned.then_inc(logit_turned, 1)
                mm.then_inc(h_summed, 1)
                pe.wait_ge(w0_lo_done, 3)
                for m in range(KD):
                    after(pe, x1_ready, KD * (c - 1) + m + 1)
                    if m == KD - 1:
                        pe.wait_ge(gates_done, c + 1)
                        for s in range(SUB):
                            mm = nc.tensor.transpose(rot[:, 2, s * P:(s + 1) * P], gate_rows[:, s].rearrange("p e r -> p (e r)"), ident[:])
                        mm.then_inc(gates_turned, 1)
                    for k in range(KD):
                        mm = product(acc[:, m], both((w0_hi, w0_lo), k, slice(m * P, (m + 1) * P)), both(X, k), k == 0, False)
                mm.then_inc(base_summed, 1)
                if not last:
                    router(slot, turn)
                pe.wait_ge(hg_lo_done, c + 1)
                for m in range(KD):
                    product(acc[:, m], both((b0_hi, b0_lo), slice(m * P, (m + 1) * P)), both((hg_hi, hg_lo)),
                            False, True).then_inc(l0_summed, 1)

            layer0_chunk(0, 0)
            layer0_chunk(0, 1)
            with pe.Fori(1, NCH // 2 - 1) as i:
                layer0_chunk(i, 0)
                layer0_chunk(i, 1)
            layer0_chunk(NCH // 2 - 1, 0)
            layer0_chunk(NCH // 2 - 1, 1, last=True)

            def half(h):
                return slice(h * HN, (h + 1) * HN)

            def a_tile(k, g, h):
                q, cols = 2 * k + g, BPC * R1
                ring, at = ((gu_hi, gu_lo), q * cols) if q < 3 * D // cols else ((dn_hi, dn_lo), q * cols - 3 * D)
                return both(ring, 0, slice(at + h * P, at + (h + 1) * P))

            def base_gu(f, g, first_only=False):
                for k in range(KD):
                    at = g * D + k * P
                    product(rot[:, (2 * f + 2 + g) % 3, :], both((gu_hi, gu_lo), (f + 1) % 2, slice(at, at + P)), both(X, k), k == 0, False)

            def lora_gu(f, g):
                for h in range(2):
                    at = 2 * D + h * 2 * P + g * P
                    mm = product(rot[:, (2 * f + 2 + g) % 3, half(h)], both((gu_hi, gu_lo), (f + 1) % 2, slice(at, at + P)),
                                 both((t_hi, t_lo), g, half(h)), False, h == 1)
                mm.then_inc(up_summed if g else gate_summed, 1)

            def down(c, f):
                s = (f + 1) % 2
                pe.wait_ge(dn_lo_done, W * c + f + 2)
                pe.wait_ge(h1_lo_done, NF * c + f + 1)
                for h in range(2):
                    at = D + h * P
                    mm = product(aux[:, half(h)], both((dn_hi, dn_lo), s, slice(at, at + P)), both((h1_hi, h1_lo), f % 2, half(h)),
                                 f == 0 and h == 0, f == NF - 1 and h == 1)
                if f == NF - 1:
                    mm.then_inc(tdn_summed, 1)
                for m in range(KD):
                    mm = product(acc[:, m], both((dn_hi, dn_lo), s, slice(m * P, (m + 1) * P)), both((h1_hi, h1_lo), f % 2),
                                 f == 0, False)
                mm.then_inc(down_summed, 1)

            def layer1_chunk(c, last=False):
                pe.wait_ge(gu_lo_done, W * c + 1)
                pe.wait_ge(dn_lo_done, W * c + 1)
                pe.wait_ge(y_lo_done, KD * c + KD)
                for g in range(2):
                    for h in range(2):
                        for k in range(KD):
                            mm = product(rot[:, g, half(h)], a_tile(k, g, h), both(X, k, half(h)), k == 0, k == KD - 1)
                    mm.then_inc(tgu_summed, 1)
                for f in range(NF):
                    pe.wait_ge(gu_lo_done, W * c + f + 2)
                    if f >= 2:
                        pe.wait_ge(h1_done, NF * c + f - 1)
                    if f == 1:
                        pe.wait_ge(t_done, T * c + 2)
                    base_gu(f, 0)
                    if f == 0:
                        pe.wait_ge(t_done, T * c + 1)
                        base_gu(f, 1)
                        pe.wait_ge(t_lo_done, T * c + 2)
                        lora_gu(f, 0)
                    else:
                        lora_gu(f, 0)
                        pe.wait_ge(silu_done, NF * c + f)
                        base_gu(f, 1)
                    lora_gu(f, 1)
                    if f == 1:
                        after(pe, out_ready, KD * c)
                    if f >= 1:
                        down(c, f - 1)
                down(c, NF - 1)
                pe.wait_ge(bd_lo_done, c + 1)
                pe.wait_ge(t_lo_done, T * c + 3)
                for m in range(KD):
                    for h in range(2):
                        mm = product(acc[:, m, half(h)], both((bd_hi, bd_lo), h, slice(m * P, (m + 1) * P)),
                                     both((t_hi, t_lo), 0, half(h)), False, h == 1)
                    mm.then_inc(out_summed, 1)

            layer1_chunk(0)
            with pe.Fori(1, NCH - 1) as c:
                layer1_chunk(c)
            layer1_chunk(NCH - 1, last=True)


def kernel(x, itok_B_0_7, itok_B_2_6, L0_cond_W, L0_cond_Wr, L0_cond_A, L0_cond_B, L1_cond_W_gate, L1_cond_W_up,
           L1_cond_W_down, L1_cond_A_gate, L1_cond_B_gate, L1_cond_A_up, L1_cond_B_up, L1_cond_A_down, L1_cond_B_down):
    import numpy as np
    import concourse.bacc as bacc
    from concourse.bass_utils import run_bass_kernel_spmd

    def rows_to_partitions(w):
        return np.ascontiguousarray(np.asarray(w).reshape(-1, P, w.shape[-1]).transpose(1, 0, 2))

    def padded(w, axis):
        w = np.asarray(w)
        pad = [(0, 0)] * w.ndim
        pad[axis] = (0, FP - F)
        return np.pad(w, pad)

    def hidden_out(w):
        return padded(w, 0).reshape(NF, P, KD, P).transpose(0, 3, 2, 1).reshape(NF, P, D)

    x = np.asarray(x)
    w1 = np.concatenate([hidden_out(L1_cond_W_gate), hidden_out(L1_cond_W_up),
                         padded(L1_cond_W_down, 1).T.reshape(NF, P, D)], axis=2)
    a_gu = np.stack([np.asarray(L1_cond_A_gate)[0], np.asarray(L1_cond_A_up)[0]])
    agu = a_gu.reshape(2, E1, R1, KD, P).transpose(1, 4, 3, 0, 2).reshape(E1, P, KD * 2, R1)
    b_gu = np.stack([padded(np.asarray(L1_cond_B_gate)[0], 1), padded(np.asarray(L1_cond_B_up)[0], 1)])
    bgu = b_gu.reshape(2, E1, NF, P, R1).transpose(1, 4, 2, 0, 3)
    adn = padded(np.asarray(L1_cond_A_down)[0], 2).reshape(E1, R1, NF, P).transpose(0, 3, 2, 1)
    bdn = np.asarray(L1_cond_B_down)[0].transpose(0, 2, 1)
    inputs = {
        "xT": x.reshape(TOK, D).T,
        "lang": np.asarray(itok_B_0_7).reshape(NCH * SUB, P // SEQ).T,
        "adapter": np.asarray(itok_B_2_6).reshape(1, BATCH),
        "w0": rows_to_partitions(np.asarray(L0_cond_W).T),
        "a0": rows_to_partitions(np.asarray(L0_cond_A).reshape(E0 * R0, D).T),
        "b0": np.asarray(L0_cond_B).transpose(0, 2, 1).reshape(E0 * R0, D),
        "wr": rows_to_partitions(np.asarray(L0_cond_Wr).T),
        "w1": w1, "agu": agu, "bgu": bgu, "adn": adn, "bdn": bdn,
    }
    inputs = {n: np.ascontiguousarray(a) for n, a in inputs.items()}
    nc = bacc.Bacc("TRN2", target_bir_lowering=False, num_devices=1)
    aps = [nc.dram_tensor(n, a.shape, mybir.dt.from_np(a.dtype), kind="ExternalInput").ap() for n, a in inputs.items()]
    out = nc.dram_tensor("outT", (D, TOK), F32, kind="ExternalOutput").ap()
    build(nc, *aps, out)
    r = run_bass_kernel_spmd(nc, [inputs], core_ids=[0])
    return np.ascontiguousarray(r.results[0]["outT"].T).reshape(BATCH, SEQ, D)
```

```python
from contextlib import ExitStack

import concourse.bass as bass
from concourse import mybir

ALU = mybir.AluOpType
ACT = mybir.ActivationFunctionType
AX_X = mybir.AxisListType.X
F32 = mybir.dt.float32
F32R = mybir.dt.float32r
I32 = mybir.dt.int32

P = 128
BATCH, SEQ, D = 128, 32, 512
TOK = BATCH * SEQ
E0, R0 = 8, 16
E1, R1 = 16, 16
F = 1376
NF = -(-F // P)
FP = NF * P
KD = D // P
N = 512
NCH = TOK // N
SUB = N // P
BPC = N // SEQ
HB = BPC // 2
HN = N // 2
GROUP = 3
NG = -(-NF // GROUP)
TILE_W = 2 * D + D
LANG_BIAS, SCALING, LORA_SCALE = 5.0, 2.0, 0.5


def build(nc, xT, lang, adapter, w0, a0, b0, wr, w1, agu, bgu, adn, bdn, outT):
    x1_dram = nc.dram_tensor("x1_scratch", (D, TOK), F32, kind="Internal").ap()
    x_v = xT.rearrange("(k p) t -> p k t", p=P)
    x1_v = x1_dram.rearrange("(k p) t -> p k t", p=P)
    out_v = outT.rearrange("(k p) t -> p k t", p=P)

    def after(eng, semaphore, n):
        if not isinstance(n, int) or n > 0:
            eng.wait_ge(semaphore, n)

    with ExitStack() as ctx:
        def sb(name, shape, dt=F32, where=ctx):
            return where.enter_context(nc.sbuf_tensor(name, shape, dt))

        def pair(name, shape, where=ctx):
            return sb(name + "_hi", shape, F32R, where), sb(name + "_lo", shape, F32R, where)

        def sem(name):
            return ctx.enter_context(nc.semaphore(name))

        w1_sb = sb("w1_sb", [P, NF, TILE_W])
        agu_sb = sb("agu_sb", [P, BPC, KD * 2, R1])
        bgu_sb = sb("bgu_sb", [P, 2, 2, GROUP, 2, P])
        adn_sb = sb("adn_sb", [P, BPC, NF, R1])
        bdn_sb = sb("bdn_sb", [P, 2, D])
        own = sb("own", [P, HB * SEQ])
        adapter_sb = sb("adapter_sb", [1, BATCH], I32)
        x_in0 = sb("x_in0", [P, KD, N])
        x_hi, x_lo = pair("x", [P, KD, N])
        y_out = sb("y_out", [P, KD, N])

        only0 = ExitStack()
        w0_sb = sb("w0_sb", [P, KD, D], where=only0)
        a0_sb = sb("a0_sb", [P, KD, P], where=only0)
        b0_sb = sb("b0_sb", [P, D], where=only0)
        h_sb = sb("h_sb", [P, N], where=only0)
        hg_sb = sb("hg_sb", [P, N], where=only0)
        logitT = sb("logitT", [2 * E0, N], where=only0)
        x_in = [x_in0, sb("x_in1", [P, KD, N], where=only0)]
        wr_sb = sb("wr_sb", [P, KD, E0], where=only0)
        wr_both = sb("wr_both", [P, KD, P], F32R, only0)
        w0_hi, w0_lo = pair("w0", [P, KD, D], only0)
        a0_hi, a0_lo = pair("a0", [P, KD, P], only0)
        b0_hi, b0_lo = pair("b0", [P, D], only0)
        hg_hi, hg_lo = pair("hg", [P, N], only0)
        ident = sb("ident", [P, P], where=only0)
        lower = sb("lower", [P, E0, E0], where=only0)
        lang_sb = sb("lang_sb", [P, NCH * SUB], I32, only0)
        expert_no = sb("expert_no", [P, E0], I32, only0)
        bias = sb("bias", [P, NCH * SUB, E0], where=only0)
        logit = sb("logit", [P, SUB, E0], where=only0)
        top = sb("top", [P, SUB], where=only0)
        ex = sb("ex", [P, SUB, E0], where=only0)
        above = sb("above", [P, SUB, E0, E0], where=only0)
        tied = sb("tied", [P, SUB, E0, E0], where=only0)
        rank = sb("rank", [P, SUB, E0], where=only0)
        den = sb("den", [P, SUB], where=only0)
        gate_rows = sb("gate_rows", [P, SUB, E0, R0], where=only0)
        only0.close()

        gu0, dn0 = pair("gu0", [P, 3 * D]), pair("dn0", [P, D + BPC * R1])
        gu1, dn1 = pair("gu1", [P, 3 * D]), pair("dn1", [P, D + BPC * R1])
        gu, dn = list(zip(gu0, gu1)), list(zip(dn0, dn1))
        bd_hi, bd_lo = pair("bd", [P, 2, D])
        t_sb = sb("t_sb", [P, 2, N])
        t_hi, t_lo = pair("t", [P, 2, N])
        silu = sb("silu", [P, 2, N])
        h1_hi, h1_lo = pair("h1", [P, 2, N])
        td_sb, td_hi, td_lo = silu[:, 1], h1_hi[:, 1], h1_lo[:, 1]

        acc = ctx.enter_context(nc.psum_tensor("acc", [P, KD, N], F32))
        rot = ctx.enter_context(nc.psum_tensor("rot", [P, 3, N], F32))
        aux = ctx.enter_context(nc.psum_tensor("aux", [P, N], F32))

        wr_landed, a0_landed, w0_landed, b0_landed = sem("wr_landed"), sem("a0_landed"), sem("w0_landed"), sem("b0_landed")
        lang_landed = sem("lang_landed")
        w1_landed, adapter_landed = sem("w1_landed"), sem("adapter_landed")
        wr_zeroed = sem("wr_zeroed")
        consts_step, consts_done = sem("consts_step"), sem("consts_done")
        w0_hi_done, w0_lo_done = sem("w0_hi_done"), sem("w0_lo_done")
        x_first_landed = [sem(f"x_first_landed{k}") for k in range(KD)]
        x_landed = [sem("x_landed0"), sem("x_landed1")]
        x_hi_done, x_lo_done = sem("x_hi_done"), sem("x_lo_done")
        h_summed, h_copied = sem("h_summed"), sem("h_copied")
        logitT_summed, logitT_copied, logit_turned = sem("logitT_summed"), sem("logitT_copied"), sem("logit_turned")
        gate_step, shifted, ex_done = sem("gate_step"), sem("shifted"), sem("ex_done")
        gates_done, gates_turned = sem("gates_done"), sem("gates_turned")
        hg_done, hg_hi_done, hg_lo_done = sem("hg_done"), sem("hg_hi_done"), sem("hg_lo_done")
        base_summed, l0_summed, x1_ready, x1_stored = sem("base_summed"), sem("l0_summed"), sem("x1_ready"), sem("x1_stored")
        y_landed, res_landed = sem("y_landed"), sem("res_landed")
        y_hi_done, y_lo_done = sem("y_hi_done"), sem("y_lo_done")
        agu_landed, adn_landed, bdn_landed = sem("agu_landed"), sem("adn_landed"), sem("bdn_landed")
        bgu_landed = [sem("bgu_landed0"), sem("bgu_landed1")]
        gu_hi_done, gu_lo_done = sem("gu_hi_done"), sem("gu_lo_done")
        dn_hi_done, dn_lo_done = sem("dn_hi_done"), sem("dn_lo_done")
        bd_hi_done, bd_lo_done = sem("bd_hi_done"), sem("bd_lo_done")
        tgu_summed, tdn_summed = sem("tgu_summed"), sem("tdn_summed")
        t_done, t_hi_done, t_lo_done = sem("t_done"), sem("t_hi_done"), sem("t_lo_done")
        gate_summed, up_summed, silu_done = sem("gate_summed"), sem("up_summed"), sem("silu_done")
        h1_done, h1_hi_done, h1_lo_done = sem("h1_done"), sem("h1_hi_done"), sem("h1_lo_done")
        down_summed, out_summed, out_ready, out_stored = sem("down_summed"), sem("out_summed"), sem("out_ready"), sem("out_stored")
        td_done, td_hi_done, td_lo_done, last_stored = sem("td_done"), sem("td_hi_done"), sem("td_lo_done"), sem("last_stored")
        ALL = 16 * BPC
        W = NF + 1

        block = ctx.enter_context(nc.Block())

        @block.sync
        def _(sp):
            def load_x(c, slot):
                sp.dma_start(x_in[slot][:], x_v[:, :, bass.ds(c * N, N)]).then_inc(x_landed[slot], 16)

            def adapters(c):
                return [sp.value_load(adapter_sb[0:1, bass.ds(c * BPC + b, 1)], min_val=0, max_val=E1 - 1) for b in range(BPC)]

            def rows(b):
                return slice(R1 * (b % HB), R1 * (b % HB + 1))

            def gather_agu(named):
                for b, e in enumerate(named):
                    sp.dma_start(agu_sb[:, b], agu[bass.ds(e, 1)].rearrange("e p q r -> (e p) q r")).then_inc(agu_landed, 16)

            def gather_adn(named):
                for b, e in enumerate(named):
                    sp.dma_start(adn_sb[:, b], adn[bass.ds(e, 1)].rearrange("e p f r -> (e p) f r")).then_inc(adn_landed, 16)

            def gather_bdn(named):
                for b, e in enumerate(named):
                    sp.dma_start(bdn_sb[rows(b), b // HB], bdn[bass.ds(e, 1)].rearrange("e r m -> (e r) m")).then_inc(bdn_landed, 16)

            def gather_bgu(named, q):
                f0, n = q * GROUP, min(GROUP, NF - q * GROUP)
                for b, e in enumerate(named):
                    src = bgu[bass.ds(e, 1), :, f0:f0 + n].rearrange("e r f g m -> (e r) f g m")
                    sp.dma_start(bgu_sb[rows(b), q % 2, b // HB, 0:n], src).then_inc(bgu_landed[q % 2], 16)

            for k in range(KD):
                sp.dma_start(x_in0[:, k], x_v[:, k, 0:N]).then_inc(x_first_landed[k], 16)
                if k == 0:
                    sp.dma_start(wr_sb[:], wr).then_inc(wr_landed, 16)
            sp.dma_start(a0_sb[:], a0).then_inc(a0_landed, 16)
            sp.dma_start(w0_sb[:], w0).then_inc(w0_landed, 16)
            for j in range(P // SEQ):
                sp.dma_start(lang_sb[SEQ * j:SEQ * (j + 1), :],
                             lang[j:j + 1].to_broadcast([SEQ, NCH * SUB])).then_inc(lang_landed, 16)
            sp.dma_start(b0_sb[:], b0).then_inc(b0_landed, 16)
            load_x(1, 1)
            sp.dma_start(adapter_sb[:], adapter).then_inc(adapter_landed, 16)
            sp.wait_ge(adapter_landed, 16)
            first = adapters(0)
            early = [lambda: gather_agu(first), lambda: gather_bgu(first, 0), lambda: gather_adn(first),
                     lambda: gather_bgu(first, 1), lambda: gather_bdn(first), lambda: None]
            for c in range(2, NCH):
                sp.wait_ge(x1_ready, KD * (c - 1))
                load_x(c, c % 2)
                early[c - 2]()

            def layer1_chunk(c, last=False):
                named = adapters(c)
                after(sp, out_stored, 16 * c)
                sp.dma_start(y_out[:], x1_v[:, :, bass.ds(c * N, N)]).then_inc(res_landed, 16)
                if not last:
                    sp.wait_ge(y_lo_done, KD * c + KD)
                    sp.dma_start(x_in0[:], x1_v[:, :, bass.ds(c * N + N, N)]).then_inc(y_landed, 16)
                sp.wait_ge(gu_lo_done, W * c + 1 + 1 * GROUP)
                gather_bgu(named, 2)
                sp.wait_ge(gu_lo_done, W * c + 1 + 2 * GROUP)
                gather_bgu(named, 3)
                if not last:
                    named = adapters(c + 1)
                    sp.wait_ge(dn_lo_done, W * c + 1)
                    gather_agu(named)
                    sp.wait_ge(gu_lo_done, W * c + 1 + 3 * GROUP)
                    gather_bgu(named, 0)
                    sp.wait_ge(gu_lo_done, W * c + W)
                    gather_bgu(named, 1)
                    sp.wait_ge(dn_lo_done, W * c + W)
                    gather_adn(named)
                    sp.wait_ge(bd_lo_done, c + 1)
                    gather_bdn(named)

            sp.wait_ge(x1_stored, 16 * (NCH - 1))
            sp.dma_start(x_in0[:], x1_v[:, :, 0:N]).then_inc(y_landed, 16)
            sp.wait_ge(x1_stored, 16 * NCH)
            layer1_chunk(0)
            with sp.Fori(1, NCH - 1) as c:
                layer1_chunk(c)
            layer1_chunk(NCH - 1, last=True)
            for m in range(KD):
                sp.wait_ge(out_ready, KD * (NCH - 1) + m + 1)
                sp.dma_start(out_v[:, m, (NCH - 1) * N:], y_out[:, m]).then_inc(last_stored, 16)
            sp.wait_ge(last_stored, 16 * KD)

        @block.gpsimd
        def _(pool):
            nc.gpsimd.memset(wr_both[:].bitcast(F32), 0.0).then_inc(wr_zeroed, 1)
            nc.gpsimd.memset(ident[:], 0.0).then_inc(consts_step, 1)
            nc.gpsimd.memset(lower[:], 1.0).then_inc(consts_step, 1)
            nc.gpsimd.memset(own[:], LORA_SCALE).then_inc(consts_step, 1)
            nc.gpsimd.iota(expert_no[:], [[1, E0]], base=0, channel_multiplier=0).then_inc(consts_done, 1)
            pool.wait_ge(consts_step, 3)
            nc.gpsimd.affine_select(out=ident[:], in_=ident[:], compare_op=ALU.not_equal, fill=1.0, base=0,
                                    pattern=[[-1, P]], channel_multiplier=1).then_inc(consts_done, 1)
            nc.gpsimd.affine_select(out=lower[:], in_=lower[:], compare_op=ALU.is_gt, fill=0.0, base=0,
                                    pattern=[[1, E0], [-1, E0]], channel_multiplier=0).then_inc(consts_done, 1)
            pool.wait_ge(w0_landed, 16)
            for f in range(NF):
                pool.dma_start(w1_sb[:, f], w1[f]).then_inc(w1_landed, 16)
            nc.gpsimd.affine_select(out=own[:], in_=own[:], compare_op=ALU.is_ge, fill=0.0, base=0,
                                    pattern=[[-R1, HB], [0, SEQ]], channel_multiplier=1).then_inc(consts_step, 1)
            pool.wait_ge(consts_step, 4)
            nc.gpsimd.affine_select(out=own[:], in_=own[:], compare_op=ALU.is_ge, fill=0.0, base=R1 - 1,
                                    pattern=[[R1, HB], [0, SEQ]], channel_multiplier=-1).then_inc(consts_done, 1)
            with pool.Fori(0, NCH) as c:
                pool.wait_ge(x1_ready, KD * c + KD)
                pool.dma_start(x1_v[:, :, bass.ds(c * N, N)], y_out[:]).then_inc(x1_stored, 16)
            with pool.Fori(0, NCH - 1) as c:
                pool.wait_ge(out_ready, KD * c + KD)
                pool.dma_start(out_v[:, :, bass.ds(c * N, N)], y_out[:]).then_inc(out_stored, 16)
            pool.wait_ge(out_stored, 16 * (NCH - 1))

        def agu_parts():
            src = agu_sb[:].rearrange("p b q r -> p q b r")
            in_gu, in_dn = 3 * D // (BPC * R1), 2
            first = [x[0][:].rearrange("p (q b r) -> p q b r", q=in_gu, b=BPC) for x in gu]
            rest = [x[0][:, 0:D].rearrange("p (q b r) -> p q b r", q=in_dn, b=BPC) for x in dn]
            return (src[:, 0:in_gu], *first), (src[:, in_gu:], *rest)

        def gu_parts(f):
            s = (f + 1) % 2
            b = bgu_sb[:, (f // GROUP) % 2, :, f % GROUP].rearrange("p h g m -> p h (g m)")
            return ((w1_sb[:, f, 0:2 * D], *[x[s][:, 0:2 * D] for x in gu]),
                    (b, *[x[s][:, 2 * D:].rearrange("p (h m) -> p h m", h=2) for x in gu]))

        def dn_parts(f):
            s = (f + 1) % 2
            return ((w1_sb[:, f, 2 * D:], *[x[s][:, 0:D] for x in dn]),
                    (adn_sb[:, :, f], *[x[s][:, D:].rearrange("p (b r) -> p b r", b=BPC) for x in dn]))

        def bgu_arrived(eng, c, f):
            q = f // GROUP
            eng.wait_ge(bgu_landed[q % 2], ALL * (2 * c + q // 2 + 1))

        @block.scalar
        def _(act):
            def his(parts, done):
                for src, hi, _ in parts:
                    ins = nc.scalar.copy(hi, src)
                ins.then_inc(done, 1)

            for k in range(KD):
                act.wait_ge(x_first_landed[k], 16)
                nc.scalar.copy(x_hi[:, k], x_in0[:, k]).then_inc(x_hi_done, 1)
                if k == 0:
                    act.wait_ge(wr_landed, 16)
                    act.wait_ge(wr_zeroed, 1)
                    nc.scalar.copy(wr_both[:, :, 0:E0], wr_sb[:]).then_inc(w0_hi_done, 1)
            act.wait_ge(a0_landed, 16)
            nc.scalar.copy(a0_hi[:], a0_sb[:]).then_inc(w0_hi_done, 1)
            act.wait_ge(logitT_summed, 1)
            nc.scalar.copy(logitT[:], rot[0:2 * E0, 1, :]).then_inc(logitT_copied, 1)
            act.wait_ge(w0_landed, 16)
            for m in range(KD):
                cols = slice(m * P, (m + 1) * P)
                nc.scalar.copy(w0_hi[:, :, cols], w0_sb[:, :, cols]).then_inc(w0_hi_done, 1)
            act.wait_ge(b0_landed, 16)
            nc.scalar.copy(b0_hi[:], b0_sb[:]).then_inc(w0_hi_done, 1)

            def layer0_chunk(i, j, last=False):
                c, slot, turn = 2 * i + j, (j + 1) % 2, i + (j + 1) // 2
                act.wait_ge(h_summed, c + 1)
                after(act, hg_done, c)
                nc.scalar.copy(h_sb[:], rot[:, 0, :]).then_inc(h_copied, 1)
                act.wait_ge(shifted, c + 1)
                nc.scalar.activation(ex[:], logit[:], ACT.Exp).then_inc(ex_done, 1)
                if last:
                    act.wait_ge(agu_landed, ALL)
                    act.wait_ge(w0_lo_done, 3 + KD)
                    his([agu_parts()[0]], gu_hi_done)
                act.wait_ge(hg_done, c + 1)
                nc.scalar.copy(hg_hi[:], hg_sb[:]).then_inc(hg_hi_done, 1)
                if not last:
                    act.wait_ge(x_landed[slot], 16 * (turn + slot))
                    act.wait_ge(base_summed, c + 1)
                    for k in range(KD):
                        nc.scalar.copy(x_hi[:, k], x_in[slot][:, k]).then_inc(x_hi_done, 1)
                    act.wait_ge(logitT_summed, c + 2)
                    nc.scalar.copy(logitT[:], rot[0:2 * E0, 1, :]).then_inc(logitT_copied, 1)

            layer0_chunk(0, 0)
            layer0_chunk(0, 1)
            with act.Fori(1, NCH // 2 - 1) as i:
                layer0_chunk(i, 0)
                layer0_chunk(i, 1)
            layer0_chunk(NCH // 2 - 1, 0)
            layer0_chunk(NCH // 2 - 1, 1, last=True)

            def y_his(c):
                act.wait_ge(y_landed, 16 * c + 16)
                for k in range(KD):
                    nc.scalar.copy(x_hi[:, k], x_in0[:, k]).then_inc(y_hi_done, 1)

            act.wait_ge(base_summed, NCH)
            y_his(0)
            act.wait_ge(hg_lo_done, NCH)
            his([agu_parts()[1]], dn_hi_done)
            act.wait_ge(x1_ready, KD * NCH)
            act.wait_ge(w1_landed, 16 * NF)
            bgu_arrived(act, 0, 0)
            his(gu_parts(0), gu_hi_done)

            def layer1_chunk(c, last=False):
                for g in range(2):
                    act.wait_ge(t_done, 2 * c + g + 1)
                    nc.scalar.copy(t_hi[:, g], t_sb[:, g]).then_inc(t_hi_done, 1)
                bgu_arrived(act, c, 1)
                his(gu_parts(1), gu_hi_done)
                for f in range(NF):
                    act.wait_ge(gate_summed, NF * c + f + 1)
                    if f >= 2:
                        act.wait_ge(h1_lo_done, NF * c + f - 1)
                    elif f == 1:
                        after(act, td_lo_done, c)
                    else:
                        after(act, h1_lo_done, NF * c)
                    nc.scalar.activation(silu[:, f % 2], rot[:, (2 * f + 2) % 3, :], ACT.Silu).then_inc(silu_done, 1)
                    act.wait_ge(h1_done, NF * c + f + 1)
                    if f >= 2:
                        act.wait_ge(down_summed, NF * c + f - 1)
                    elif f == 1:
                        after(act, out_summed, KD * c)
                    else:
                        after(act, down_summed, NF * c)
                    nc.scalar.copy(h1_hi[:, f % 2], silu[:, f % 2]).then_inc(h1_hi_done, 1)
                    if f == 0:
                        after(act, down_summed, NF * c)
                        act.wait_ge(adn_landed, ALL * c + ALL)
                        his(dn_parts(0), dn_hi_done)
                    if f + 2 < NF:
                        bgu_arrived(act, c, f + 2)
                        his(gu_parts(f + 2), gu_hi_done)
                    if f == 8:
                        act.wait_ge(bdn_landed, ALL * c + ALL)
                        after(act, out_summed, KD * c)
                        nc.scalar.copy(bd_hi[:], bdn_sb[:]).then_inc(bd_hi_done, 1)
                    if f == NF - 2 and not last:
                        act.wait_ge(agu_landed, ALL * c + 2 * ALL)
                        his([agu_parts()[0]], gu_hi_done)
                    if f < NF - 1:
                        if f >= 1:
                            act.wait_ge(down_summed, NF * c + f)
                        his(dn_parts(f + 1), dn_hi_done)
                if not last:
                    y_his(c + 1)
                    act.wait_ge(down_summed, NF * c + NF - 1)
                    his([agu_parts()[1]], dn_hi_done)
                act.wait_ge(td_done, c + 1)
                nc.scalar.copy(td_hi, td_sb).then_inc(td_hi_done, 1)
                if not last:
                    bgu_arrived(act, c + 1, 0)
                    his(gu_parts(0), gu_hi_done)

            layer1_chunk(0)
            with act.Fori(1, NCH - 1) as c:
                layer1_chunk(c)
            layer1_chunk(NCH - 1, last=True)

        @block.vector
        def _(dve):
            G = 12

            def lo(out, x, hi, done):
                nc.vector.tensor_tensor(out, x, hi.bitcast(F32), ALU.subtract).then_inc(done, 1)

            def los(parts, done):
                for src, hi, low in parts:
                    ins = nc.vector.tensor_tensor(low, src, hi.bitcast(F32), ALU.subtract)
                ins.then_inc(done, 1)

            for k in range(KD):
                dve.wait_ge(x_hi_done, k + 1)
                lo(x_lo[:, k], x_in0[:, k], x_hi[:, k], x_lo_done)
                if k == 0:
                    dve.wait_ge(w0_hi_done, 1)
                    lo(wr_both[:, :, E0:2 * E0], wr_sb[:], wr_both[:, :, 0:E0], w0_lo_done)
            dve.wait_ge(w0_hi_done, 2)
            lo(a0_lo[:], a0_sb[:], a0_hi[:], w0_lo_done)
            for m in range(KD):
                dve.wait_ge(w0_hi_done, 3 + m)
                cols = slice(m * P, (m + 1) * P)
                lo(w0_lo[:, :, cols], w0_sb[:, :, cols], w0_hi[:, :, cols], w0_lo_done)
            dve.wait_ge(lang_landed, 16 * (P // SEQ))
            dve.wait_ge(consts_done, 3)
            nc.vector.tensor_tensor(bias[:], lang_sb[:].unsqueeze(2).to_broadcast([P, NCH * SUB, E0]),
                                    expert_no[:].unsqueeze(1).to_broadcast([P, NCH * SUB, E0]),
                                    ALU.is_equal).then_inc(gate_step, 1)
            dve.wait_ge(gate_step, 1)
            nc.vector.tensor_scalar(bias[:], bias[:], LANG_BIAS, None, ALU.mult).then_inc(gate_step, 1)

            dve.wait_ge(w0_hi_done, 3 + KD)
            lo(b0_lo[:], b0_sb[:], b0_hi[:], w0_lo_done)

            def y_los(c):
                for k in range(KD):
                    dve.wait_ge(y_hi_done, KD * c + k + 1)
                    lo(x_lo[:, k], x_in0[:, k], x_hi[:, k], y_lo_done)

            def layer0_chunk(i, j, last=False):
                c, slot = 2 * i + j, (j + 1) % 2
                g0 = G * c + 2
                dve.wait_ge(gate_step, g0)
                dve.wait_ge(logit_turned, c + 1)
                shares = aux[:, 0:SUB * 2 * E0].rearrange("p (s two e) -> p s two e", s=SUB, two=2)
                nc.vector.tensor_tensor(logit[:], shares[:, :, 1], bias[:, bass.ds(c * SUB, SUB), :],
                                        ALU.add).then_inc(gate_step, 1)
                dve.wait_ge(gate_step, g0 + 1)
                nc.vector.tensor_tensor(logit[:], logit[:], shares[:, :, 0], ALU.add).then_inc(gate_step, 1)
                dve.wait_ge(gate_step, g0 + 2)
                nc.vector.tensor_reduce(top[:], logit[:], AX_X, ALU.max).then_inc(gate_step, 1)
                mine = logit[:].unsqueeze(3).to_broadcast([P, SUB, E0, E0])
                others = logit[:].unsqueeze(2).to_broadcast([P, SUB, E0, E0])
                nc.vector.tensor_tensor(above[:], others, mine, ALU.is_gt).then_inc(gate_step, 1)
                nc.vector.tensor_tensor(tied[:], others, mine, ALU.is_equal).then_inc(gate_step, 1)
                dve.wait_ge(gate_step, g0 + 5)
                nc.vector.tensor_tensor(logit[:], logit[:], top[:].unsqueeze(2).to_broadcast([P, SUB, E0]),
                                        ALU.subtract).then_inc(shifted, 1)
                nc.vector.tensor_tensor(tied[:], tied[:], lower[:].unsqueeze(1).to_broadcast([P, SUB, E0, E0]),
                                        ALU.mult).then_inc(gate_step, 1)
                dve.wait_ge(gate_step, g0 + 6)
                nc.vector.tensor_tensor(above[:], above[:], tied[:], ALU.add).then_inc(gate_step, 1)
                dve.wait_ge(gate_step, g0 + 7)
                nc.vector.tensor_reduce(rank[:], above[:], AX_X, ALU.add).then_inc(gate_step, 1)
                dve.wait_ge(gate_step, g0 + 8)
                dve.wait_ge(ex_done, c + 1)
                nc.vector.scalar_tensor_tensor(out=ex[:], in0=rank[:], scalar=1.5, in1=ex[:], op0=ALU.is_lt,
                                               op1=ALU.mult).then_inc(gate_step, 1)
                dve.wait_ge(gate_step, g0 + 9)
                nc.vector.tensor_reduce(den[:], ex[:], AX_X, ALU.add).then_inc(gate_step, 1)
                dve.wait_ge(gate_step, g0 + 10)
                nc.vector.reciprocal(den[:], den[:]).then_inc(gate_step, 1)
                dve.wait_ge(gate_step, g0 + 11)
                nc.vector.tensor_tensor(ex[:], ex[:], den[:].unsqueeze(2).to_broadcast([P, SUB, E0]),
                                        ALU.mult).then_inc(gate_step, 1)
                dve.wait_ge(gate_step, g0 + 12)
                nc.vector.tensor_scalar(gate_rows[:], ex[:].unsqueeze(3).to_broadcast([P, SUB, E0, R0]),
                                        SCALING, None, ALU.mult).then_inc(gates_done, 1)
                if last:
                    dve.wait_ge(gu_hi_done, 1)
                    los([agu_parts()[0]], gu_lo_done)
                dve.wait_ge(gates_turned, c + 1)
                dve.wait_ge(h_copied, c + 1)
                nc.vector.tensor_tensor(hg_sb[:], h_sb[:], rot[:, 2, :], ALU.mult).then_inc(hg_done, 1)
                dve.wait_ge(hg_hi_done, c + 1)
                lo(hg_lo[:], hg_sb[:], hg_hi[:], hg_lo_done)
                if not last:
                    for k in range(KD):
                        dve.wait_ge(x_hi_done, KD * c + KD + k + 1)
                        lo(x_lo[:, k], x_in[slot][:, k], x_hi[:, k], x_lo_done)
                else:
                    y_los(0)
                    dve.wait_ge(dn_hi_done, 1)
                    los([agu_parts()[1]], dn_lo_done)
                after(dve, x1_stored, 16 * c)
                for m in range(KD):
                    dve.wait_ge(l0_summed, KD * c + m + 1)
                    nc.vector.tensor_tensor(y_out[:, m], x_in[j][:, m], acc[:, m], ALU.add).then_inc(x1_ready, 1)

            layer0_chunk(0, 0)
            layer0_chunk(0, 1)
            with dve.Fori(1, NCH // 2 - 1) as i:
                layer0_chunk(i, 0)
                layer0_chunk(i, 1)
            layer0_chunk(NCH // 2 - 1, 0)
            layer0_chunk(NCH // 2 - 1, 1, last=True)

            dve.wait_ge(gu_hi_done, 2)
            los(gu_parts(0), gu_lo_done)
            dve.wait_ge(consts_done, 4)
            halves = own[:].unsqueeze(1).to_broadcast([P, 2, HN])

            def low_rank_gu(c):
                for g in range(2):
                    dve.wait_ge(tgu_summed, 2 * c + g + 1)
                    nc.vector.tensor_tensor(t_sb[:, g].rearrange("p (h t) -> p h t", h=2),
                                            rot[:, g, :].rearrange("p (h t) -> p h t", h=2), halves,
                                            ALU.mult).then_inc(t_done, 1)
                for g in range(2):
                    dve.wait_ge(t_hi_done, 2 * c + g + 1)
                    lo(t_lo[:, g], t_sb[:, g], t_hi[:, g], t_lo_done)

            low_rank_gu(0)

            def layer1_chunk(c, last=False):
                dve.wait_ge(gu_hi_done, W * c + 3)
                los(gu_parts(1), gu_lo_done)
                for f in range(NF):
                    s = silu[:, f % 2]
                    dve.wait_ge(silu_done, NF * c + f + 1)
                    dve.wait_ge(up_summed, NF * c + f + 1)
                    nc.vector.tensor_tensor(s, s, rot[:, (2 * f + 3) % 3, :], ALU.mult).then_inc(h1_done, 1)
                    dve.wait_ge(h1_hi_done, NF * c + f + 1)
                    lo(h1_lo[:, f % 2], s, h1_hi[:, f % 2], h1_lo_done)
                    if f == 0:
                        dve.wait_ge(dn_hi_done, W * c + 2)
                        los(dn_parts(0), dn_lo_done)
                    if f + 2 < NF:
                        dve.wait_ge(gu_hi_done, W * c + f + 4)
                        los(gu_parts(f + 2), gu_lo_done)
                    if f == 8:
                        dve.wait_ge(bd_hi_done, c + 1)
                        lo(bd_lo[:], bdn_sb[:], bd_hi[:], bd_lo_done)
                    if f == NF - 2 and not last:
                        dve.wait_ge(gu_hi_done, W * c + W + 1)
                        los([agu_parts()[0]], gu_lo_done)
                    if f < NF - 1:
                        dve.wait_ge(dn_hi_done, W * c + f + 3)
                        los(dn_parts(f + 1), dn_lo_done)
                if not last:
                    y_los(c + 1)
                    dve.wait_ge(dn_hi_done, W * c + W + 1)
                    los([agu_parts()[1]], dn_lo_done)
                dve.wait_ge(tdn_summed, c + 1)
                nc.vector.tensor_tensor(td_sb.rearrange("p (h t) -> p h t", h=2),
                                        aux[:].rearrange("p (h t) -> p h t", h=2), halves,
                                        ALU.mult).then_inc(td_done, 1)
                dve.wait_ge(td_hi_done, c + 1)
                lo(td_lo, td_sb, td_hi, td_lo_done)
                if not last:
                    dve.wait_ge(gu_hi_done, W * c + W + 2)
                    los(gu_parts(0), gu_lo_done)
                    low_rank_gu(c + 1)
                dve.wait_ge(res_landed, 16 * c + 16)
                for m in range(KD):
                    dve.wait_ge(out_summed, KD * c + m + 1)
                    nc.vector.tensor_tensor(y_out[:, m], y_out[:, m], acc[:, m], ALU.add).then_inc(out_ready, 1)

            layer1_chunk(0)
            with dve.Fori(1, NCH - 1) as c:
                layer1_chunk(c)
            layer1_chunk(NCH - 1, last=True)

        @block.tensor
        def _(pe):
            def product(out, w, x, first, last):
                (wh, wl), (xh, xl) = w, x
                nc.tensor.matmul(out, wh, xh, start=first, stop=False, skip_group_check=True)
                nc.tensor.matmul(out, wh, xl, start=False, stop=False, skip_group_check=True)
                return nc.tensor.matmul(out, wl, xh, start=False, stop=last, skip_group_check=True)

            def both(operand, *index):
                return tuple(x[(slice(None), *index)] for x in operand)

            X = (x_hi, x_lo)

            def router(c):
                for k in range(KD):
                    pe.wait_ge(x_lo_done, KD * c + k + 1)
                    nc.tensor.matmul(rot[:, 1, :], wr_both[:, k], x_hi[:, k], start=(k == 0), stop=False)
                    mm = nc.tensor.matmul(rot[:, 1, :], wr_both[:, k], x_lo[:, k], start=False, stop=(k == KD - 1))
                mm.then_inc(logitT_summed, 1)

            pe.wait_ge(w0_lo_done, 1)
            router(0)

            def layer0_chunk(i, j, last=False):
                c = 2 * i + j
                first = isinstance(c, int) and c == 0
                if first:
                    pe.wait_ge(w0_lo_done, 2)
                for k in range(KD):
                    if k == 2:
                        if first:
                            pe.wait_ge(consts_done, 3)
                        pe.wait_ge(logitT_copied, c + 1)
                    mm = product(rot[:, 0, :], both((a0_hi, a0_lo), k), both(X, k), k == 0, k == KD - 1)
                    if k == 2:
                        for s in range(SUB):
                            turned = nc.tensor.transpose(aux[:, 2 * E0 * s:2 * E0 * (s + 1)], logitT[:, s * P:(s + 1) * P],
                                                         ident[0:2 * E0, 0:2 * E0])
                        turned.then_inc(logit_turned, 1)
                mm.then_inc(h_summed, 1)
                for m in range(KD):
                    if first:
                        pe.wait_ge(w0_lo_done, 3 + m)
                    after(pe, x1_ready, KD * (c - 1) + m + 1)
                    if m == KD - 1:
                        pe.wait_ge(gates_done, c + 1)
                        for s in range(SUB):
                            mm = nc.tensor.transpose(rot[:, 2, s * P:(s + 1) * P], gate_rows[:, s].rearrange("p e r -> p (e r)"), ident[:])
                        mm.then_inc(gates_turned, 1)
                    for k in range(KD):
                        mm = product(acc[:, m], both((w0_hi, w0_lo), k, slice(m * P, (m + 1) * P)), both(X, k), k == 0, False)
                mm.then_inc(base_summed, 1)
                if first:
                    pe.wait_ge(w0_lo_done, 3 + KD)
                pe.wait_ge(hg_lo_done, c + 1)
                for m in range(KD):
                    product(acc[:, m], both((b0_hi, b0_lo), slice(m * P, (m + 1) * P)), both((hg_hi, hg_lo)),
                            False, True).then_inc(l0_summed, 1)
                if not last:
                    router(c + 1)

            layer0_chunk(0, 0)
            layer0_chunk(0, 1)
            with pe.Fori(1, NCH // 2 - 1) as i:
                layer0_chunk(i, 0)
                layer0_chunk(i, 1)
            layer0_chunk(NCH // 2 - 1, 0)
            layer0_chunk(NCH // 2 - 1, 1, last=True)

            def half(h):
                return slice(h * HN, (h + 1) * HN)

            def a_tile(k, g, h):
                q, cols = 2 * k + g, BPC * R1
                ring, at = (gu0, q * cols) if q < 3 * D // cols else (dn0, q * cols - 3 * D)
                return both(ring, slice(at + h * P, at + (h + 1) * P))

            def base_gu(f, g):
                for k in range(KD):
                    at = g * D + k * P
                    product(rot[:, (2 * f + 2 + g) % 3, :], both((gu0, gu1)[(f + 1) % 2], slice(at, at + P)), both(X, k), k == 0, False)

            def lora_gu(f, g):
                for h in range(2):
                    at = 2 * D + h * 2 * P + g * P
                    mm = product(rot[:, (2 * f + 2 + g) % 3, half(h)], both((gu0, gu1)[(f + 1) % 2], slice(at, at + P)),
                                 both((t_hi, t_lo), g, half(h)), False, h == 1)
                mm.then_inc(up_summed if g else gate_summed, 1)

            def down(c, f):
                w = (dn0, dn1)[(f + 1) % 2]
                pe.wait_ge(dn_lo_done, W * c + f + 2)
                pe.wait_ge(h1_lo_done, NF * c + f + 1)
                for h in range(2):
                    at = D + h * P
                    mm = product(aux[:, half(h)], both(w, slice(at, at + P)), both((h1_hi, h1_lo), f % 2, half(h)),
                                 f == 0 and h == 0, f == NF - 1 and h == 1)
                if f == NF - 1:
                    mm.then_inc(tdn_summed, 1)
                for m in range(KD):
                    mm = product(acc[:, m], both(w, slice(m * P, (m + 1) * P)), both((h1_hi, h1_lo), f % 2),
                                 f == 0, False)
                mm.then_inc(down_summed, 1)

            def low_rank_gu(c):
                pe.wait_ge(gu_lo_done, W * c + 1)
                pe.wait_ge(dn_lo_done, W * c + 1)
                pe.wait_ge(y_lo_done, KD * c + KD)
                for g in range(2):
                    for h in range(2):
                        for k in range(KD):
                            mm = product(rot[:, g, half(h)], a_tile(k, g, h), both(X, k, half(h)), k == 0, k == KD - 1)
                    mm.then_inc(tgu_summed, 1)

            low_rank_gu(0)

            def layer1_chunk(c, last=False):
                for f in range(NF):
                    pe.wait_ge(gu_lo_done, W * c + f + 2)
                    if f >= 2:
                        pe.wait_ge(h1_done, NF * c + f - 1)
                    if f == 1:
                        pe.wait_ge(t_done, 2 * c + 2)
                    base_gu(f, 0)
                    if f == 0:
                        pe.wait_ge(t_done, 2 * c + 1)
                        base_gu(f, 1)
                        pe.wait_ge(t_lo_done, 2 * c + 2)
                        lora_gu(f, 0)
                    else:
                        lora_gu(f, 0)
                        pe.wait_ge(silu_done, NF * c + f)
                        base_gu(f, 1)
                    lora_gu(f, 1)
                    if f == 1:
                        after(pe, out_ready, KD * c)
                    if f >= 1:
                        down(c, f - 1)
                down(c, NF - 1)
                if not last:
                    low_rank_gu(c + 1)
                pe.wait_ge(bd_lo_done, c + 1)
                pe.wait_ge(td_lo_done, c + 1)
                for m in range(KD):
                    for h in range(2):
                        mm = product(acc[:, m, half(h)], both((bd_hi, bd_lo), h, slice(m * P, (m + 1) * P)),
                                     (td_hi[:, half(h)], td_lo[:, half(h)]), False, h == 1)
                    mm.then_inc(out_summed, 1)

            layer1_chunk(0)
            with pe.Fori(1, NCH - 1) as c:
                layer1_chunk(c)
            layer1_chunk(NCH - 1, last=True)


def kernel(x, itok_B_0_7, itok_B_2_6, L0_cond_W, L0_cond_Wr, L0_cond_A, L0_cond_B, L1_cond_W_gate, L1_cond_W_up,
           L1_cond_W_down, L1_cond_A_gate, L1_cond_B_gate, L1_cond_A_up, L1_cond_B_up, L1_cond_A_down, L1_cond_B_down):
    import numpy as np
    import concourse.bacc as bacc
    from concourse.bass_utils import run_bass_kernel_spmd

    def rows_to_partitions(w):
        return np.ascontiguousarray(np.asarray(w).reshape(-1, P, w.shape[-1]).transpose(1, 0, 2))

    def padded(w, axis):
        w = np.asarray(w)
        pad = [(0, 0)] * w.ndim
        pad[axis] = (0, FP - F)
        return np.pad(w, pad)

    def hidden_out(w):
        return padded(w, 0).reshape(NF, P, KD, P).transpose(0, 3, 2, 1).reshape(NF, P, D)

    x = np.asarray(x)
    w1 = np.concatenate([hidden_out(L1_cond_W_gate), hidden_out(L1_cond_W_up),
                         padded(L1_cond_W_down, 1).T.reshape(NF, P, D)], axis=2)
    a_gu = np.stack([np.asarray(L1_cond_A_gate)[0], np.asarray(L1_cond_A_up)[0]])
    agu = a_gu.reshape(2, E1, R1, KD, P).transpose(1, 4, 3, 0, 2).reshape(E1, P, KD * 2, R1)
    b_gu = np.stack([padded(np.asarray(L1_cond_B_gate)[0], 1), padded(np.asarray(L1_cond_B_up)[0], 1)])
    bgu = b_gu.reshape(2, E1, NF, P, R1).transpose(1, 4, 2, 0, 3)
    adn = padded(np.asarray(L1_cond_A_down)[0], 2).reshape(E1, R1, NF, P).transpose(0, 3, 2, 1)
    bdn = np.asarray(L1_cond_B_down)[0].transpose(0, 2, 1)
    inputs = {
        "xT": x.reshape(TOK, D).T,
        "lang": np.asarray(itok_B_0_7).reshape(NCH * SUB, P // SEQ).T,
        "adapter": np.asarray(itok_B_2_6).reshape(1, BATCH),
        "w0": rows_to_partitions(np.asarray(L0_cond_W).T),
        "a0": rows_to_partitions(np.asarray(L0_cond_A).reshape(E0 * R0, D).T),
        "b0": np.asarray(L0_cond_B).transpose(0, 2, 1).reshape(E0 * R0, D),
        "wr": rows_to_partitions(np.asarray(L0_cond_Wr).T),
        "w1": w1, "agu": agu, "bgu": bgu, "adn": adn, "bdn": bdn,
    }
    inputs = {n: np.ascontiguousarray(a) for n, a in inputs.items()}
    nc = bacc.Bacc("TRN2", target_bir_lowering=False, num_devices=1)
    aps = [nc.dram_tensor(n, a.shape, mybir.dt.from_np(a.dtype), kind="ExternalInput").ap() for n, a in inputs.items()]
    out = nc.dram_tensor("outT", (D, TOK), F32, kind="ExternalOutput").ap()
    build(nc, *aps, out)
    r = run_bass_kernel_spmd(nc, [inputs], core_ids=[0])
    return np.ascontiguousarray(r.results[0]["outT"].T).reshape(BATCH, SEQ, D)
```
